# Optimizing a Trainium2 kernel written in Bass

```python
import numpy as np
import jax
import jax.numpy as jnp

def _softmax(x, axis=-1):
    return jax.nn.softmax(x, axis=axis)

def _gelu(x):
    return jax.nn.gelu(x, approximate=True)

def _silu(x):
    return jax.nn.silu(x)

def _sigmoid(x):
    return jax.nn.sigmoid(x)

def _layernorm(x, axis=-1, eps=1e-05):
    m = jnp.mean(x, axis=axis, keepdims=True)
    v = jnp.var(x, axis=axis, keepdims=True)
    return (x - m) / jnp.sqrt(v + eps)

def _scatter_add(tgt, idx, src, axis=0):
    return tgt.at[idx].add(src)

def _segment_sum(src, seg, n):
    return jax.ops.segment_sum(src, seg, n)
kernel_name = 'mk_xattn_ffn_d1_seqx_r2_a7e938'

def setup_inputs(seed: int=0):
    np.random.seed(seed)
    _w = jnp.asarray

    def _rec_inputs():
        import jax
        import jax.numpy as jnp
        _rk = jax.random.key(seed)
        x = -0.0002928 + 1 * jax.random.normal(jax.random.fold_in(_rk, 1), (8, 1024, 512), jnp.float32)
        _lenS = 1024 - jax.random.randint(jax.random.fold_in(_rk, 7), (8,), 0, max(1, 1024 // 4) + 1, jnp.int32)
        _lenS2 = 64 - jax.random.randint(jax.random.fold_in(_rk, 8), (8,), 0, max(1, 64 // 4) + 1, jnp.int32)
        _ctx_1024P = jax.random.normal(jax.random.fold_in(_rk, 11), (8, 16, 512), jnp.float32)
        _ctx_1024c = jax.random.dirichlet(jax.random.fold_in(_rk, 511), 0.3 * jnp.ones((16,), jnp.float32), (8, 64))
        _ctx_1024t = jnp.einsum('bsk,bkd->bsd', _ctx_1024c, _ctx_1024P)
        _ctx_1024t = _ctx_1024t * jax.lax.rsqrt(jnp.mean(jnp.square(_ctx_1024t)) + 1e-12) * 0.953939
        ctx_1024 = 4.13588e-05 + 0.999923 * (_ctx_1024t + 0.3 * jax.random.normal(jax.random.fold_in(_rk, 611), (8, 64, 512), jnp.float32))
        return (x, ctx_1024)
    x, ctx_1024 = _rec_inputs()

    def _L0_xattn_setup():
        import jax, jax.numpy as jnp
        import numpy as np
        EMBED_DIM = 512
        NUM_HEADS = 16
        HEAD_DIM = EMBED_DIM // NUM_HEADS
        key = jax.random.key(seed)
        ks = jax.random.split(key, 11)
        B, Q, K = (4, 512, 1024)
        s = 1.0 / np.sqrt(EMBED_DIM)
        return {'query': jax.random.normal(ks[0], (B, Q, EMBED_DIM), jnp.float32), 'key': jax.random.normal(ks[1], (B, K, EMBED_DIM), jnp.float32), 'value': jax.random.normal(ks[2], (B, K, EMBED_DIM), jnp.float32), 'Wq': jax.random.normal(ks[3], (EMBED_DIM, EMBED_DIM), jnp.float32) * s, 'bq': jnp.zeros((EMBED_DIM,), jnp.float32), 'Wk': jax.random.normal(ks[4], (EMBED_DIM, EMBED_DIM), jnp.float32) * s, 'bk': jnp.zeros((EMBED_DIM,), jnp.float32), 'Wv': jax.random.normal(ks[5], (EMBED_DIM, EMBED_DIM), jnp.float32) * s, 'bv': jnp.zeros((EMBED_DIM,), jnp.float32), 'Wo': jax.random.normal(ks[6], (EMBED_DIM, EMBED_DIM), jnp.float32) * s, 'bo': jnp.zeros((EMBED_DIM,), jnp.float32)}
    _L0_xattn_all = _L0_xattn_setup()
    _L0_xattn_in = {k: v for k, v in _L0_xattn_all.items() if k in ('Wq', 'bq', 'Wk', 'bk', 'Wv', 'bv', 'Wo', 'bo')}
    del _L0_xattn_all

    def _L0_ffn_setup():
        import jax, jax.numpy as jnp
        import numpy as np
        B, N, D = (4, 1024, 512)
        SPARSITY = 0.01
        key = jax.random.key(seed)
        k1, k2, k3 = jax.random.split(key, 3)
        x = jax.random.normal(k1, (B, N, D), dtype=jnp.float32)
        spatial = jax.random.normal(k2, (D, D), dtype=jnp.float32) * 0.02
        freq = jnp.fft.fft(spatial, axis=-1)
        k = int(D * SPARSITY)
        mag = jnp.abs(freq)
        kth = jax.lax.top_k(mag, k)[0][:, -1:]
        w_sparse = jnp.where(mag >= kth, freq, 0.0 + 0j)
        bias = jax.random.normal(k3, (D,), dtype=jnp.float32) * 0.01
        return {'x': x, 'w_freq_real': jnp.real(w_sparse).astype(jnp.float32), 'w_freq_imag': jnp.imag(w_sparse).astype(jnp.float32), 'bias': bias}
    _L0_ffn_all = _L0_ffn_setup()
    _L0_ffn_in = {k: v for k, v in _L0_ffn_all.items() if k in ('w_freq_real', 'w_freq_imag', 'bias')}
    del _L0_ffn_all
    return {'x': x, 'ctx_1024': ctx_1024, 'L0_xattn_Wq': _L0_xattn_in['Wq'], 'L0_xattn_bq': _L0_xattn_in['bq'], 'L0_xattn_Wk': _L0_xattn_in['Wk'], 'L0_xattn_bk': _L0_xattn_in['bk'], 'L0_xattn_Wv': _L0_xattn_in['Wv'], 'L0_xattn_bv': _L0_xattn_in['bv'], 'L0_xattn_Wo': _L0_xattn_in['Wo'], 'L0_xattn_bo': _L0_xattn_in['bo'], 'L0_ffn_w_freq_real': _L0_ffn_in['w_freq_real'], 'L0_ffn_w_freq_imag': _L0_ffn_in['w_freq_imag'], 'L0_ffn_bias': _L0_ffn_in['bias']}

def reference(x, ctx_1024, L0_xattn_Wq, L0_xattn_bq, L0_xattn_Wk, L0_xattn_bk, L0_xattn_Wv, L0_xattn_bv, L0_xattn_Wo, L0_xattn_bo, L0_ffn_w_freq_real, L0_ffn_w_freq_imag, L0_ffn_bias):
    import jax
    import jax.numpy as jnp

    def _L0_xattn_ref(query, key, value, Wq, bq, Wk, bk, Wv, bv, Wo, bo):
        import jax, jax.numpy as jnp
        import numpy as np
        EMBED_DIM = 512
        NUM_HEADS = 16
        HEAD_DIM = EMBED_DIM // NUM_HEADS
        B = query.shape[0]
        q = query @ Wq.T + bq
        k = key @ Wk.T + bk
        v = value @ Wv.T + bv
        q = q.reshape(B, -1, NUM_HEADS, HEAD_DIM)
        k = k.reshape(B, -1, NUM_HEADS, HEAD_DIM)
        v = v.reshape(B, -1, NUM_HEADS, HEAD_DIM)
        scores = jnp.einsum('bqhd,bkhd->bhqk', q, k) / np.sqrt(HEAD_DIM).astype(np.float32)
        probs = jax.nn.softmax(scores, axis=-1)
        out = jnp.einsum('bhqk,bkhd->bqhd', probs, v)
        out = out.reshape(B, -1, EMBED_DIM)
        return out @ Wo.T + bo

    def _L0_ffn_ref(x, w_freq_real, w_freq_imag, bias):
        import jax, jax.numpy as jnp
        import numpy as np
        B, N, D = (4, 1024, 512)
        SPARSITY = 0.01
        w = jax.lax.complex(w_freq_real, w_freq_imag)
        x_freq = jnp.fft.fft(x, axis=-1)
        y_freq = jnp.einsum('bnd,do->bno', x_freq, w)
        y = jnp.real(jnp.fft.ifft(y_freq, axis=-1))
        return y + bias
    x = x + _L0_xattn_ref(_layernorm(x, axis=-1), ctx_1024, ctx_1024, L0_xattn_Wq, L0_xattn_bq, L0_xattn_Wk, L0_xattn_bk, L0_xattn_Wv, L0_xattn_bv, L0_xattn_Wo, L0_xattn_bo)
    x = x + _L0_ffn_ref(_layernorm(x, axis=-1), L0_ffn_w_freq_real, L0_ffn_w_freq_imag, L0_ffn_bias)
    return x

_drawn_inputs = setup_inputs


def setup_inputs(seed=0):
    import zlib

    import numpy as np

    out = dict(_drawn_inputs(seed))
    spreads = {'L0_xattn_bq': (0.0, 0.394),
     'L0_xattn_bk': (0.0, 0.8),
     'L0_xattn_bv': (0.0, 0.1),
     'L0_xattn_bo': (0.0, 0.1)}
    factors = {'L0_ffn_bias': 8.0}
    for name, (base, spread) in spreads.items():
        noise = np.random.default_rng([zlib.crc32(name.encode()), seed]).standard_normal(out[name].shape)
        drawn = base * np.exp(spread * noise) if base else spread * noise
        out[name] = jnp.asarray(drawn.astype(out[name].dtype))
    for name, factor in factors.items():
        out[name] = (out[name] * factor).astype(out[name].dtype)
    return out
```

```python
from contextlib import ExitStack

import numpy as np

import concourse.bass as bass
from concourse import mybir

F32 = mybir.dt.float32
F32R = mybir.dt.float32r
F16 = mybir.dt.float16
I32 = mybir.dt.int32
ALU = mybir.AluOpType
ACT = mybir.ActivationFunctionType
AX = mybir.AxisListType
RMAX = bass.bass_isa.ReduceOp.max

P = 128
EPS = 1e-5
HIGH, LOW = 0, 1
PASSES = ((HIGH, HIGH), (HIGH, LOW), (LOW, HIGH))
EXPONENT_BITS = 0x7F800000
LN_GAIN = 10
TOP = 13
P_GAIN = 14

STAT1, NORM1, PAIR = -5, -4, -2
VALUES, PROJECT, FORWARD, RESULT = 1, 2, 3, 4


def tables(D):
    a = 2 * (P * np.arange(D // 2 // P)[None, None, :, None] + np.arange(P)[:, None, None, None]) \
        + np.arange(2)[None, :, None, None]
    angle = 2 * np.pi * ((a * np.arange(D // 2)) % D) / D
    return np.stack([np.cos(angle), np.sin(angle)], axis=1).astype(np.float32)


def xattn_ffn_kernel(nc, x, ctx, Wq, bq, Wk, bk, Wv, bv, Wo, bo, w_real, w_imag, bias, cos_sin, identity, out):
    B, S, D = x.shape
    KEYS = ctx.shape[1]
    HEADS = 16
    HD = D // HEADS
    C = D // P
    HALF = D // 2
    PAIRS = HEADS // 2
    HPC = P // HD
    TPB = S // P
    TILES = B * TPB
    TG = 4
    VW = 2 * HD + 2
    SCALE = 1.0 / float(np.sqrt(np.float32(HD)))
    assert TPB == 8 and C == 4 and KEYS * 2 == P and B * KEYS == D and B > 2

    x_groups = x.rearrange("b (g p t) f -> (b g) p t f", p=P, t=TG)
    out_groups = out.rearrange("b (g p t) f -> (b g) p t f", p=P, t=TG)

    stack = ExitStack()
    with stack:
        def sb(name, shape, dt, where=stack):
            return where.enter_context(nc.sbuf_tensor(name, shape, dt))

        def ps(name, shape):
            return stack.enter_context(nc.psum_tensor(name, shape, F32))

        def sem(name):
            return stack.enter_context(nc.semaphore(name))

        key_blocks = sb("key_blocks", [P, 2, B, C, HPC * KEYS], F16)
        value_blocks = sb("value_blocks", [P, 2, B, PAIRS, VW], F16)
        WqT = sb("WqT", [P, 2, C, C, P], F16)
        WoT = sb("WoT", [P, 2, C, C, P], F16)
        ffn = sb("ffn", [P, 2, C, D], F16)
        bo_rows = sb("bo_rows", [P, D], F32)
        bias_rows = sb("bias_rows", [P, D], F32)
        ident = sb("ident", [P, P], F32)
        bias_cols = sb("bias_cols", [P, 3, C], F32)
        peaks = sb("peaks", [P, 3, 8], F32)
        powers = sb("powers", [P, 8], F32)
        gains = sb("gains", [P, 3, 8], F32)
        factors = sb("factors", [P, 4], F32)
        minus_half = sb("minus_half", [P, 1], F32)
        wide = sb("wide", [P, C, D], F32)

        early = ExitStack()
        turned = sb("turned", [P, 2, 2, C, D], F32R, early)
        spectra = turned
        trig = sb("trig", [P, 3, 2, 2, 2, HALF], F32R, early)
        odd = sb("odd", [P, 2, HALF], F32, early)
        sums = sb("sums", [P, 2, D], F32, early)
        columns = sb("columns", [P, 2, 2, 2, 2, 2, P], F32R, early)
        raw = sb("raw", [P, 3, C, D], F32, early)
        keys = sb("keys", [P, C, D], F32, early)
        parts = sb("parts", [P, 2, C, D], F16, early)
        bv_rows = sb("bv_rows", [P, D], F32, early)
        early.close()

        q_sum = sb("q_sum", [P, 2, 2, 2 * P], F32)
        q = sb("q", [P, 2, 2, C, 2 * P], F16)
        shifted = sb("shifted", [P, HEADS, KEYS], F32)
        prob = sb("prob", [P, HEADS * KEYS], F32)
        prob_parts = sb("prob_parts", [P, 2, 2, HEADS * KEYS], F16)
        probT = sb("probT", [P, 2, 2, PAIRS, P], F16)
        o_rows = sb("o_rows", [P, 2, D], F32)
        o_parts = sb("o_parts", [P, 2, 2, D], F16)
        oT = sb("oT", [P, 2, 2, C, P], F16)
        n2 = sb("n2", [P, 2, D], F32)
        n2_parts = sb("n2_parts", [P, 2, 2, D], F16)
        n2T = sb("n2T", [P, 2, 2, C, P], F16)
        most = sb("most", [P, 2, HEADS], F32)
        per_sum = sb("per_sum", [P, 2, HEADS], F32)
        stats = sb("stats", [P, 2, 2, 6], F32)
        moments = sb("moments", [P, 2, 4, 2], F32)
        vareps = sb("vareps", [P, 2, 4], F32)
        rstd = sb("rstd", [P, 2, 4], F32)
        rows = sb("rows", [P, 4, TG, D], F32)
        n1 = sb("n1", [P, 2, D], F32)
        n1_parts = sb("n1_parts", [P, 2, 2, 2, D], F16)
        n1T = sb("n1T", [P, 2, 2, 2, C, P], F16)

        ps_q = ps("ps_q", [P, 2, 2 * P])
        ps_proj = ps("ps_proj", [P, D])
        ps_ffn = ps("ps_ffn", [P, D])
        ps_spare = ps("ps_spare", [P, D])
        ps_s = ps("ps_s", [P, 2, D])
        ps_o = ps("ps_o", [P, PAIRS, P])
        banks = [ps_q[:].rearrange("p a b -> p (a b)"),
                 ps_proj[:], ps_ffn[:], ps_spare[:], ps_s[:, 0, :], ps_s[:, 1, :],
                 ps_o[:, 0:4, :].rearrange("p a b -> p (a b)"), ps_o[:, 4:8, :].rearrange("p a b -> p (a b)")]

        ctx_in, wk_in, wv_in, trig_in, ident_in = map(sem, ("ctx_in", "wk_in", "wv_in", "trig_in", "ident_in"))
        real_in, imag_in, wq_in, wo_in = map(sem, ("real_in", "imag_in", "wq_in", "wo_in"))
        cols_in, bv_in, rows_in = map(sem, ("cols_in", "bv_in", "rows_in"))
        turn_made, key_made, value_made, g_made, a_made = map(sem, ("turn_made", "key_made", "value_made", "g_made", "a_made"))
        turn_hi, turn_lo, key_kept, value_kept = map(sem, ("turn_hi", "turn_lo", "key_kept", "value_kept"))
        trig_hi, trig_lo, trig_neg, cols_hi, cols_lo = map(sem, ("trig_hi", "trig_lo", "trig_neg", "cols_hi", "cols_lo"))
        g_odd, g_sum, g_hi, g_lo, a_odd, a_sum = map(sem, ("g_odd", "g_sum", "g_hi", "g_lo", "a_odd", "a_sum"))
        peak_own, peak_all, gain_ready, chain = map(sem, ("peak_own", "peak_all", "gain_ready", "chain"))
        bound_ready, query_ready = map(sem, ("bound_ready", "query_ready"))
        part_hi, part_lo, weight_turned, keys_spread, values_spread = map(
            sem, ("part_hi", "part_lo", "weight_turned", "keys_spread", "values_spread"))
        filled, ones_set, ffn_hi, ffn_lo = map(sem, ("filled", "ones_set", "ffn_hi", "ffn_lo"))
        bn1, mv1, ve1, rs1, n1_made, n1_hi, n1_lo = map(sem, ("bn1", "mv1", "ve1", "rs1", "n1_made", "n1_hi", "n1_lo"))
        q_made, q_kept, q_hi, q_lo = map(sem, ("q_made", "q_kept", "q_hi", "q_lo"))
        s_made, s_max, s_shifted, p_made, p_hi, p_lo = map(
            sem, ("s_made", "s_max", "s_shifted", "p_made", "p_hi", "p_lo"))
        o_made, o_rec, o_kept, o_hi, o_lo = map(sem, ("o_made", "o_rec", "o_kept", "o_hi", "o_lo"))
        proj_made, xb_made, x2_made, bn2, mv2, ve2, rs2 = map(
            sem, ("proj_made", "xb_made", "x2_made", "bn2", "mv2", "ve2", "rs2"))
        n2_made, n2_hi, n2_lo, ffn_made, x2b_made, y_made = map(
            sem, ("n2_made", "n2_hi", "n2_lo", "ffn_made", "x2b_made", "y_made"))
        x_in, y_out, n1_turned, p_turned, o_turned, n2_turned = (
            [sem(f"{name}_{turn}") for turn in range(2)]
            for name in ("x_in", "y_out", "n1_turned", "p_turned", "o_turned", "n2_turned"))

        def due(eng, *waits, alone=False):
            waits = [(semaphore, value) for semaphore, value in waits if not isinstance(value, int) or value > 0]
            if alone and any(not isinstance(value, int) for _, value in waits):
                waits = [(semaphore, value if isinstance(value, int) else eng.to_reg(value)) for semaphore, value in waits]
                eng.wait_ge(waits[0][0], 1)
            for semaphore, value in waits:
                eng.wait_ge(semaphore, value)

        def steps(eng, step, first=STAT1 - 2):
            for k in range(first, TPB):
                step(0, k)
            with eng.Fori(1, B - 1) as b:
                for k in range(TPB):
                    step(b, k)
            for k in range(TPB * (B - 1), TILES + RESULT):
                step(0, k)

        def on(b, k):
            return not isinstance(b, int) or 0 <= k < TILES

        def at(b, k):
            return b * TPB + k

        def row_tile(b, k):
            group = k // TG
            return rows[:, ((b + group // 2) % 2) * 2 + group % 2, k % TG, :]

        PQ, PB, PK, PV, PO, PA, PBIAS = range(7)
        SCORES, PROJ, FFN, QUERY = range(4)

        block = stack.enter_context(nc.Block())

        def rounds(b, t, each=TPB):
            return b * (each // 2) + t // 2

        @block.sync
        def _(sp):
            weight_rows = "(r p) f -> p r f"
            spectrum_rows = "(c p a) o -> a p c o"
            sp.dma_start(raw[:, 0], ctx.rearrange("b k f -> (b k) f").rearrange(weight_rows, p=P)).then_inc(ctx_in, 16)
            sp.dma_start(ident[:], identity).then_inc(ident_in, 16)
            sp.dma_start(raw[:, 1], Wk.rearrange(weight_rows, p=P)).then_inc(wk_in, 16)
            with nc.allow_non_contiguous_dma(reason="two biases as columns, 4 KB"):
                sp.dma_start(bias_cols[:, 0, :], bq.rearrange("(c p) -> p c", p=P)).then_inc(cols_in, 16)
                sp.dma_start(bias_cols[:, 1, :], bk.rearrange("(c p) -> p c", p=P)).then_inc(cols_in, 16)
            sp.dma_start(wide[:].rearrange("p r n -> p (r n)"), cos_sin).then_inc(trig_in, 16)
            sp.dma_start(raw[:, 2], Wv.rearrange(weight_rows, p=P)).then_inc(wv_in, 16)
            sp.dma_start(bv_rows[:], bv.partition_broadcast(P)).then_inc(bv_in, 16)
            sp.dma_start(bo_rows[:], bo.partition_broadcast(P)).then_inc(rows_in, 16)
            sp.dma_start(bias_rows[:], bias.partition_broadcast(P)).then_inc(rows_in, 16)
            sp.wait_ge(turn_made, C)
            for a in range(2):
                sp.dma_start(raw[:, 0, 2 * a:2 * a + 2, :], w_real.rearrange(spectrum_rows, p=P, a=2)[a]).then_inc(real_in, 16)
            sp.wait_ge(turn_made, 2 * C)
            for a in range(2):
                sp.dma_start(raw[:, 1, 2 * a:2 * a + 2, :], w_imag.rearrange(spectrum_rows, p=P, a=2)[a]).then_inc(imag_in, 16)
            sp.wait_ge(turn_made, 3 * C)
            sp.dma_start(raw[:, 2], Wq.rearrange(weight_rows, p=P)).then_inc(wq_in, 16)
            for n, turned_weight in enumerate((WqT, WoT)):
                sp.wait_ge(part_lo, 3 + n)
                if n == 0:
                    sp.dma_start(raw[:, 2], Wo.rearrange(weight_rows, p=P)).then_inc(wo_in, 16)
                sp.dma_start_transpose(turned_weight[:].rearrange("p a r c o -> p (a r c) o"),
                                       parts[:].rearrange("p a r f -> p (a r f)")).then_inc(weight_turned, 16)
            sp.wait_ge(g_made, 2 * C)
            sp.wait_ge(weight_turned, 32)
            sp.wait_ge(g_hi, 2 * C)
            sp.wait_ge(g_lo, 2 * C)

            def step(b, k):
                if on(b, k - FORWARD):
                    t = k - FORWARD
                    due(sp, (n2_lo, at(b, t) + 1),
                            (ffn_made, at(b, t) - 1), alone=True)
                    sp.dma_start_transpose(n2T[:, t % 2].rearrange("p a c n -> p (a c) n"),
                                           n2_parts[:, t % 2].rearrange("p a f -> p (a f)")).then_inc(n2_turned[t % 2], 16)
                if (k - RESULT) % TG == TG - 1 and on(b, k - RESULT):
                    t = k - RESULT
                    due(sp, (y_made, at(b, t) + 1), alone=True)
                    group = t // TG
                    sp.dma_start(out_groups[b * (TPB // TG) + group],
                                 rows[:, ((b + group // 2) % 2) * 2 + group % 2]).then_inc(y_out[group % 2], 16)
                if (k - STAT1 + 2) % TG == 0 and on(b, k - STAT1 + 2):
                    group = (k - STAT1 + 2) // TG
                    due(sp, (y_out[group % 2], rounds(b, group - 4, TPB // TG) * 16 + 16), alone=True)
                    sp.dma_start(rows[:, ((b + group // 2) % 2) * 2 + group % 2],
                                 x_groups[b * (TPB // TG) + group]).then_inc(x_in[group % 2], 16)
                if (k - NORM1) % 2 == 1 and on(b, k - NORM1):
                    t = k - NORM1
                    ring = (t // 2) % 2
                    due(sp, (n1_lo, at(b, t) + 1),
                            (q_made, at(b, t) - 3), alone=True)
                    sp.dma_start_transpose(n1T[:, ring].rearrange("p a t c n -> p (a t c) n"),
                                           n1_parts[:, ring].rearrange("p a t f -> p (a t f)")).then_inc(n1_turned[ring], 16)
                if on(b, k - VALUES):
                    t = k - VALUES
                    due(sp, (o_lo, at(b, t) + 1),
                            (proj_made, at(b, t) - 1), alone=True)
                    sp.dma_start_transpose(oT[:, t % 2].rearrange("p a c n -> p (a c) n"),
                                           o_parts[:, t % 2].rearrange("p a f -> p (a f)")).then_inc(o_turned[t % 2], 16)
                if on(b, k):
                    due(sp, (p_lo, at(b, k) + 1),
                            (o_made, at(b, k) - 1), alone=True)
                    sp.dma_start_transpose(probT[:, k % 2].rearrange("p a g n -> p (a g) n"),
                                           prob_parts[:, k % 2].rearrange("p a f -> p (a f)")).then_inc(p_turned[k % 2], 16)

            steps(sp, step)
            for done in y_out:
                sp.wait_ge(done, TILES // TG // 2 * 16)

        @block.gpsimd
        def _(pool):
            pool.memset(minus_half[:], -0.5).then_inc(filled, 1)
            pool.memset(value_blocks[:].rearrange("p a b g w -> p (a b g w)").bitcast(F32), 0.0).then_inc(filled, 1)
            pool.memset(key_blocks[:].rearrange("p a b c w -> p (a b c w)").bitcast(F32), 0.0).then_inc(filled, 1)
            pool.wait_ge(filled, 3)
            for head in range(2):
                rows_of = slice(head * KEYS, head * KEYS + KEYS)
                pool.memset(value_blocks[rows_of, HIGH, :, :, 2 * HD + head:2 * HD + head + 1], 1.0).then_inc(ones_set, 1)
            pool.wait_ge(ones_set, 2)

            peaks_seen = [0]

            def peak_of_all(col):
                peaks_seen[0] += 1
                pool.wait_ge(peak_own, peaks_seen[0])
                pool.partition_all_reduce(peaks[:, 1, col:col + 1], peaks[:, 0, col:col + 1], P, RMAX).then_inc(peak_all, 1)

            def rest(to, whole, high):
                return pool.tensor_tensor(to, whole, high, ALU.subtract)

            peak_of_all(PBIAS)
            peak_of_all(PK)
            for n in range(4):
                for which in range(2):
                    pool.wait_ge(cols_hi, 2 * n + which + 1)
                    rest(columns[:, n % 2, which, LOW].rearrange("p a c o -> p (a c) o"),
                         raw[:, which].rearrange("p r (o a) -> p r o a", a=2)[:, :, P * (n % 2):P * (n % 2) + P, n // 2],
                         columns[:, n % 2, which, HIGH].rearrange("p a c o -> p (a c) o").bitcast(F32)).then_inc(cols_lo, 1)
                if n < 3:
                    peak_of_all((PV, PQ, PO)[n])

            def deviation(b, t, moments_made, sum_made, done, norm):
                slot = slice(t % 4, t % 4 + 1)
                due(pool, (moments_made, at(b, t) + 1), alone=True)
                pool.tensor_scalar(vareps[:, norm, slot], moments[:, norm, t % 4, 1:2], EPS, 2.0 ** (-2 * LN_GAIN),
                                   ALU.add, ALU.mult).then_inc(sum_made, 1)
                due(pool, (sum_made, at(b, t) + 1), alone=True)
                pool.tensor_tensor(rstd[:, norm, slot], vareps[:, norm, slot], minus_half[:], ALU.pow).then_inc(done, 1)

            def step(b, k):
                if on(b, k - FORWARD):
                    t = k - FORWARD
                    due(pool, (n2_hi, at(b, t) + 1), alone=True)
                    rest(n2_parts[:, t % 2, LOW], n2[:, t % 2], n2_parts[:, t % 2, HIGH]).then_inc(n2_lo, 1)
                if on(b, k - STAT1):
                    deviation(b, k - STAT1, mv1, ve1, rs1, 0)
                if on(b, k - FORWARD):
                    t = k - FORWARD
                    due(pool, (n2_made, at(b, t) + 1), alone=True)
                    row = row_tile(b, t)
                    pool.tensor_tensor(row, row, bias_rows[:], ALU.add).then_inc(x2b_made, 1)
                if on(b, k - NORM1):
                    t = k - NORM1
                    due(pool, (n1_hi, at(b, t) + 1), alone=True)
                    rest(n1_parts[:, (t // 2) % 2, LOW, t % 2], n1[:, t % 2],
                         n1_parts[:, (t // 2) % 2, HIGH, t % 2]).then_inc(n1_lo, 1)
                    if k == NORM1:
                        pool.wait_ge(rows_in, 32)
                    row = row_tile(b, t)
                    pool.tensor_tensor(row, row, bo_rows[:], ALU.add).then_inc(xb_made, 1)
                if on(b, k - PAIR):
                    t = k - PAIR
                    due(pool, (q_hi, at(b, t) + 1), alone=True)
                    half = slice(2 * (t % 2), 2 * (t % 2) + 2)
                    rest(q[:, (t // 2) % 2, LOW, half], q_sum[:, t % 2], q[:, (t // 2) % 2, HIGH, half]).then_inc(q_lo, 1)
                if on(b, k - PROJECT):
                    deviation(b, k - PROJECT, mv2, ve2, rs2, 1)

            for k in range(STAT1 - 2, -2):
                step(0, k)
            peak_of_all(PA)
            steps(pool, step, first=-2)

        @block.scalar
        def _(act):
            def high(to, whole, col=None):
                if col is None:
                    return act.activation(to, whole, ACT.Copy)
                return act.activation(to, whole, ACT.Identity, bias=0.0, scale=gains[:, 1, col:col + 1])

            def turn(n):
                act.wait_ge(turn_made, n + 1)
                high(turned[:, min(n // C, 1), HIGH, n % C], banks[n % 8 if n < 8 else 4 + n % C]).then_inc(turn_hi, 1)

            for n in range(2 * C):
                turn(n)
            act.wait_ge(trig_in, 16)
            tables_in = wide[:].rearrange("p (t r) n -> p t (r n)", t=2)
            trig_flat = trig[:].rearrange("p t s a c n -> p t s (a c n)")
            high(trig_flat[:, 0:2, HIGH], tables_in).then_inc(trig_hi, 1)
            act.wait_ge(cols_in, 32)
            for j in range(C):
                act.wait_ge(key_made, j + 1)
                act.activation(keys[:, j], banks[j], ACT.Identity, bias=bias_cols[:, 1, j:j + 1]).then_inc(key_kept, 1)
            for n in range(2 * C, 3 * C):
                turn(n)
            act.wait_ge(trig_hi, 1)
            act.mul(trig_flat[:, 2, HIGH], trig_flat[:, 0, HIGH].bitcast(F32), -1.0)
            act.wait_ge(trig_lo, 1)
            act.mul(trig_flat[:, 2, LOW], trig_flat[:, 0, LOW].bitcast(F32), -1.0).then_inc(trig_neg, 1)

            def column_parts(n):
                if n == 0:
                    act.wait_ge(real_in, 32)
                    act.wait_ge(imag_in, 32)
                if n >= 2:
                    act.wait_ge(g_made, 2 * n - 2)
                for which in range(2):
                    high(columns[:, n % 2, which, HIGH].rearrange("p a c o -> p (a c) o"),
                         raw[:, which].rearrange("p r (o a) -> p r o a", a=2)[:, :, P * (n % 2):P * (n % 2) + P, n // 2]
                         ).then_inc(cols_hi, 1)

            def spectrum(n):
                bank = banks[(4 + n) % 8]
                act.wait_ge(g_made, n + 1)
                if n >= 2:
                    act.wait_ge(g_sum, 2 * n - 2)
                act.activation(odd[:, n % 2], bank[:, HALF:], ACT.Copy).then_inc(g_odd, 1)
                act.wait_ge(g_sum, 2 * n + 2)
                if n == 0:
                    act.wait_ge(value_made, C)
                high(spectra[:, n % 2, HIGH, n // 2], sums[:, n % 2]).then_inc(g_hi, 1)

            def split(n, whole, col):
                act.wait_ge(gain_ready, n + 1)
                high(parts[:, HIGH], whole, col).then_inc(part_hi, 1)

            column_parts(0)
            column_parts(1)
            split(0, keys[:], PK)
            spectrum(0)
            spectrum(1)
            column_parts(2)
            act.wait_ge(keys_spread, 8)
            split(1, wide[:], PV)
            spectrum(2)
            spectrum(3)
            column_parts(3)
            act.wait_ge(values_spread, 8)
            split(2, raw[:, 2], PQ)
            spectrum(4)
            spectrum(5)
            act.wait_ge(weight_turned, 16)
            split(3, raw[:, 2], PO)
            spectrum(6)
            spectrum(7)

            def matrix(n):
                act.wait_ge(a_made, n + 1)
                if n >= 2:
                    act.wait_ge(a_sum, 2 * n - 2)
                act.activation(odd[:, n % 2], banks[4 + n][:, HALF:], ACT.Copy).then_inc(a_odd, 1)

            def step(b, k):
                if on(b, k - FORWARD):
                    t = k - FORWARD
                    due(act, (n2_made, at(b, t) + 1))
                    due(act, (n2_turned[t % 2], rounds(b, t) * 16))
                    high(n2_parts[:, t % 2, HIGH], n2[:, t % 2]).then_inc(n2_hi, 1)
                if on(b, k - NORM1):
                    t = k - NORM1
                    due(act, (n1_made, at(b, t) + 1))
                    due(act, (n1_turned[t // 2 % 2], rounds(b, t // 2, TPB // 2) * 16))
                    high(n1_parts[:, (t // 2) % 2, HIGH, t % 2], n1[:, t % 2]).then_inc(n1_hi, 1)
                if on(b, k):
                    if k == 0 and isinstance(b, int):
                        act.wait_ge(query_ready, 2)
                    due(act, (s_shifted, at(b, k) + 1))
                    due(act, (p_lo, at(b, k)))
                    act.activation(prob[:], shifted[:].rearrange("p h n -> p (h n)"), ACT.Exp,
                                   scale=factors[:, SCORES:SCORES + 1]).then_inc(p_made, 1)
                    act.wait_ge(p_made, at(b, k) + 1)
                    due(act, (p_turned[k % 2], rounds(b, k) * 16))
                    act.activation(prob_parts[:, k % 2, HIGH], prob[:], ACT.Copy, scale=2.0 ** P_GAIN).then_inc(p_hi, 1)
                if on(b, k - PAIR):
                    t = k - PAIR
                    if k == PAIR:
                        act.wait_ge(query_ready, 2)
                    due(act, (q_made, at(b, t) + 1))
                    due(act, (q_lo, at(b, t) - 1))
                    for i in range(2):
                        j = 2 * (t % 2) + i
                        last = act.activation(q_sum[:, t % 2, i], ps_q[:, i], ACT.Identity,
                                              bias=bias_cols[:, 2, j:j + 1], scale=factors[:, QUERY:QUERY + 1])
                    last.then_inc(q_kept, 1)
                    act.wait_ge(q_kept, at(b, t) + 1)
                    due(act, (s_made, at(b, t // 2 * 2) - 2))
                    high(q[:, (t // 2) % 2, HIGH, 2 * (t % 2):2 * (t % 2) + 2], q_sum[:, t % 2]).then_inc(q_hi, 1)
                if on(b, k - VALUES):
                    t = k - VALUES
                    due(act, (o_kept, at(b, t) + 1))
                    due(act, (o_turned[t % 2], rounds(b, t) * 16))
                    high(o_parts[:, t % 2, HIGH], o_rows[:, t % 2]).then_inc(o_hi, 1)

            for n in range(C):
                matrix(n)
            for k in range(STAT1 - 2, -2):
                step(0, k)
            act.wait_ge(gain_ready, 5)
            high(ffn[:, HIGH], wide[:], PA).then_inc(ffn_hi, 1)
            steps(act, step, first=-2)

        @block.vector
        def _(dve):
            links = [0]

            def link(instruction):
                links[0] += 1
                instruction.then_inc(chain, 1)
                dve.wait_ge(chain, links[0])

            def rest(to, whole, high):
                return dve.tensor_tensor(to, whole, high, ALU.subtract)

            def turn(n):
                dve.wait_ge(turn_hi, n + 1)
                rest(turned[:, min(n // C, 1), LOW, n % C], banks[n % 8 if n < 8 else 4 + n % C],
                     turned[:, min(n // C, 1), HIGH, n % C].bitcast(F32)).then_inc(turn_lo, 1)

            def own_peak(col, whole):
                dve.tensor_reduce(peaks[:, 0, col:col + 1], whole, AX.X, ALU.max,
                                  apply_absolute_value=True).then_inc(peak_own, 1)

            def power(col, number, clipped=False):
                if not clipped:
                    dve.wait_ge(peak_all, number)
                    link(dve.tensor_scalar(peaks[:, 2, col:col + 1], peaks[:, 1, col:col + 1], 1e-30, None, ALU.max))
                link(dve.tensor_scalar(powers[:, col:col + 1].bitcast(I32), peaks[:, 2, col:col + 1].bitcast(I32),
                                       EXPONENT_BITS, None, ALU.bitwise_and))
                link(dve.reciprocal(gains[:, 0, col:col + 1], powers[:, col:col + 1]))

            def gain(col):
                dve.tensor_scalar(gains[:, 1, col:col + 1], gains[:, 0, col:col + 1], 2.0 ** TOP, None,
                                  ALU.mult).then_inc(gain_ready, 1)

            def split_rest(n, to, whole, high, col, hi_done, lo_done):
                dve.wait_ge(hi_done, n + 1)
                dve.scalar_tensor_tensor(out=to, in0=whole, scalar=gains[:, 1, col:col + 1], in1=high,
                                         op0=ALU.mult, op1=ALU.subtract).then_inc(lo_done, 1)

            for n in range(2 * C):
                turn(n)
            dve.wait_ge(trig_hi, 1)
            tables_in = wide[:].rearrange("p (t r) n -> p t (r n)", t=2)
            trig_flat = trig[:].rearrange("p t s a c n -> p t s (a c n)")
            rest(trig_flat[:, 0:2, LOW], tables_in, trig_flat[:, 0:2, HIGH].bitcast(F32)).then_inc(trig_lo, 1)
            dve.wait_ge(cols_in, 32)
            own_peak(PBIAS, bias_cols[:, 0, :])
            dve.wait_ge(key_kept, C)
            own_peak(PK, keys[:].rearrange("p c n -> p (c n)"))
            for n in range(2 * C, 3 * C):
                turn(n)
            power(PK, 2)
            gain(PK)
            dve.wait_ge(bv_in, 16)
            dve.wait_ge(trig_lo, 1)
            for r in range(C):
                dve.wait_ge(value_made, r + 1)
                dve.tensor_tensor(wide[:, r], banks[r], bv_rows[:], ALU.add).then_inc(value_kept, 1)

            def spread_keys():
                dve.wait_ge(filled, 3)
                dve.wait_ge(part_lo, 1)
                for part in range(2):
                    for h in range(HPC):
                        of = slice(HD * h, HD * h + HD)
                        dve.tensor_copy(key_blocks[of, part, :, :, KEYS * h:KEYS * h + KEYS],
                                        parts[of, part].rearrange("p c (b n) -> p b c n", b=B)).then_inc(keys_spread, 1)

            def spread_values():
                dve.wait_ge(ones_set, 2)
                dve.wait_ge(part_lo, 2)
                for part in range(2):
                    for b in range(2):
                        for h in range(2):
                            dve.tensor_copy(
                                value_blocks[KEYS * h:KEYS * h + KEYS, part, b::2, :, HD * h:HD * h + HD],
                                parts[KEYS * b:KEYS * b + KEYS, part].rearrange("p r (g h d) -> p r g h d", h=2, d=HD)[:, :, :, h]
                            ).then_inc(values_spread, 1)

            def spectrum(n):
                bank = banks[(4 + n) % 8]
                dve.wait_ge(g_odd, n + 1)
                if n >= 2:
                    dve.wait_ge(g_hi, n - 1)
                for half, op in enumerate((ALU.add, ALU.subtract)):
                    dve.tensor_tensor(sums[:, n % 2, HALF * half:HALF * half + HALF], bank[:, :HALF], odd[:, n % 2],
                                      op).then_inc(g_sum, 1)
                dve.wait_ge(g_hi, n + 1)
                rest(spectra[:, n % 2, LOW, n // 2], sums[:, n % 2],
                     spectra[:, n % 2, HIGH, n // 2].bitcast(F32)).then_inc(g_lo, 1)

            spectrum(0)
            dve.wait_ge(value_kept, C)
            own_peak(PV, wide[:].rearrange("p c n -> p (c n)"))
            split_rest(0, parts[:, LOW], keys[:], parts[:, HIGH], PK, part_hi, part_lo)
            spectrum(1)
            spread_keys()
            power(PV, 3)
            gain(PV)
            spectrum(2)
            split_rest(1, parts[:, LOW], wide[:], parts[:, HIGH], PV, part_hi, part_lo)
            dve.wait_ge(wq_in, 16)
            own_peak(PQ, raw[:, 2].rearrange("p c n -> p (c n)"))
            spectrum(3)
            power(PBIAS, 1)
            power(PQ, 4)
            spread_values()
            gain(PQ)
            link(dve.scalar_tensor_tensor(out=peaks[:, 2, PB:PB + 1], in0=peaks[:, 2, PQ:PQ + 1], scalar=float(D),
                                          in1=peaks[:, 2, PBIAS:PBIAS + 1], op0=ALU.mult, op1=ALU.add))
            power(PB, 0, clipped=True)
            link(dve.tensor_scalar(gains[:, 1, PB:PB + 1], gains[:, 0, PB:PB + 1], 2.0 ** (TOP + 1), None, ALU.mult))
            dve.tensor_scalar(bias_cols[:, 2, :], bias_cols[:, 0, :], gains[:, 1, PB:PB + 1], None, ALU.mult)
            dve.tensor_scalar(factors[:, QUERY:QUERY + 1], powers[:, PQ:PQ + 1], gains[:, 1, PB:PB + 1],
                              2.0 ** -(TOP + LN_GAIN), ALU.mult, ALU.mult).then_inc(query_ready, 1)
            dve.tensor_scalar(factors[:, SCORES:SCORES + 1], powers[:, PB:PB + 1], powers[:, PK:PK + 1],
                              SCALE * 2.0 ** -(2 * TOP + 1), ALU.mult, ALU.mult).then_inc(query_ready, 1)
            spectrum(4)
            split_rest(2, parts[:, LOW], raw[:, 2], parts[:, HIGH], PQ, part_hi, part_lo)
            dve.wait_ge(wo_in, 16)
            own_peak(PO, raw[:, 2].rearrange("p c n -> p (c n)"))
            spectrum(5)
            power(PO, 5)
            gain(PO)
            link(dve.tensor_scalar(factors[:, PROJ:PROJ + 1], powers[:, PV:PV + 1], powers[:, PO:PO + 1],
                                   2.0 ** -(2 * TOP), ALU.mult, ALU.mult))
            spectrum(6)
            split_rest(3, parts[:, LOW], raw[:, 2], parts[:, HIGH], PO, part_hi, part_lo)
            spectrum(7)

            def stat(row, t, first_done, done, norm, count):
                dve.bn_stats(stats[:, norm, t % 2], row).then_inc(first_done, 1)
                due(dve, (first_done, count), alone=True)
                dve.bn_aggr(moments[:, norm, t % 4], stats[:, norm, t % 2]).then_inc(done, 1)

            def normal(to, row, t, norm):
                return dve.tensor_scalar(to, row, moments[:, norm, t % 4, 0:1], rstd[:, norm, t % 4:t % 4 + 1],
                                         ALU.subtract, ALU.mult)

            def step(b, k):
                if on(b, k - RESULT):
                    t = k - RESULT
                    row = row_tile(b, t)
                    due(dve, (ffn_made, at(b, t) + 1))
                    due(dve, (x2b_made, at(b, t) + 1))
                    dve.scalar_tensor_tensor(out=row, in0=ps_ffn[:], scalar=factors[:, FFN:FFN + 1], in1=row,
                                             op0=ALU.mult, op1=ALU.add).then_inc(y_made, 1)
                if on(b, k - FORWARD):
                    t = k - FORWARD
                    due(dve, (rs2, at(b, t) + 1))
                    due(dve, (n2_lo, at(b, t) - 1))
                    normal(n2[:, t % 2], row_tile(b, t), t, 1).then_inc(n2_made, 1)
                if on(b, k - NORM1):
                    t = k - NORM1
                    due(dve, (rs1, at(b, t) + 1))
                    due(dve, (n1_lo, at(b, t) - 1))
                    normal(n1[:, t % 2], row_tile(b, t), t, 0).then_inc(n1_made, 1)
                if on(b, k):
                    due(dve, (s_made, at(b, k) + 1))
                    scores = ps_s[:].rearrange("p a (h n) -> p (a h) n", n=KEYS)
                    dve.tensor_reduce(most[:, k % 2], scores, AX.X, ALU.max).then_inc(s_max, 1)
                    dve.wait_ge(s_max, at(b, k) + 1)
                    due(dve, (p_made, at(b, k)))
                    dve.tensor_tensor(shifted[:], scores, most[:, k % 2].unsqueeze(2).to_broadcast([P, HEADS, KEYS]),
                                      ALU.subtract).then_inc(s_shifted, 1)
                if on(b, k - STAT1):
                    t = k - STAT1
                    if t % TG == 0:
                        due(dve, (x_in[t // TG % 2], rounds(b, t // TG, TPB // TG) * 16 + 16), alone=True)
                    stat(row_tile(b, t), t, bn1, mv1, 0, at(b, t) + 1)
                if on(b, k - VALUES):
                    t = k - VALUES
                    due(dve, (o_made, at(b, t) + 1))
                    dve.reciprocal(per_sum[:, t % 2].rearrange("p (g h) -> p g h", h=2),
                                   ps_o[:, :, 2 * HD:VW]).then_inc(o_rec, 1)
                    dve.wait_ge(o_rec, at(b, t) + 1)
                    due(dve, (o_lo, at(b, t) - 1))
                    dve.tensor_tensor(
                        o_rows[:, t % 2].rearrange("p (g h d) -> p g h d", h=2, d=HD),
                        ps_o[:, :, 0:2 * HD].rearrange("p g (h d) -> p g h d", h=2),
                        per_sum[:, t % 2].rearrange("p (g h) -> p g h", h=2).unsqueeze(3).to_broadcast([P, PAIRS, 2, HD]),
                        ALU.mult).then_inc(o_kept, 1)
                if on(b, k):
                    due(dve, (p_hi, at(b, k) + 1))
                    dve.scalar_tensor_tensor(out=prob_parts[:, k % 2, LOW], in0=prob[:], scalar=2.0 ** P_GAIN,
                                             in1=prob_parts[:, k % 2, HIGH], op0=ALU.mult,
                                             op1=ALU.subtract).then_inc(p_lo, 1)
                if on(b, k - VALUES):
                    t = k - VALUES
                    due(dve, (o_hi, at(b, t) + 1))
                    rest(o_parts[:, t % 2, LOW], o_rows[:, t % 2], o_parts[:, t % 2, HIGH]).then_inc(o_lo, 1)
                if on(b, k - PROJECT):
                    t = k - PROJECT
                    row = row_tile(b, t)
                    due(dve, (proj_made, at(b, t) + 1))
                    due(dve, (xb_made, at(b, t) + 1))
                    dve.scalar_tensor_tensor(out=row, in0=ps_proj[:], scalar=factors[:, PROJ:PROJ + 1], in1=row,
                                             op0=ALU.mult, op1=ALU.add).then_inc(x2_made, 1)
                    due(dve, (x2_made, at(b, t) + 1), alone=True)
                    stat(row, t, bn2, mv2, 1, at(b, t) + 1)

            for n in range(C):
                dve.wait_ge(a_odd, n + 1)
                for half, op in enumerate((ALU.add, ALU.subtract)):
                    if n == 0 and half == 0:
                        dve.wait_ge(part_lo, 2)
                    dve.tensor_tensor(wide[:, n, HALF * half:HALF * half + HALF], banks[4 + n][:, :HALF], odd[:, n % 2],
                                      op).then_inc(a_sum, 1)
            for k in range(STAT1 - 2, -2):
                step(0, k)
            dve.wait_ge(a_sum, 2 * C)
            own_peak(PA, wide[:].rearrange("p c n -> p (c n)"))
            power(PA, 6)
            gain(PA)
            split_rest(0, ffn[:, LOW], wide[:], ffn[:, HIGH], PA, ffn_hi, ffn_lo)
            link(dve.tensor_scalar(factors[:, FFN:FFN + 1], powers[:, PA:PA + 1], 2.0 ** -(TOP + LN_GAIN) / D, None, ALU.mult))
            steps(dve, step, first=-2)

        @block.tensor
        def _(pe):
            def turn(n, slot):
                for r in range(C):
                    last = pe.transpose(banks[n % 8 if n < 8 else 4 + n % C][:, P * r:P * r + P],
                                        raw[:, slot, r, P * (n % C):P * (n % C) + P], ident[:])
                last.then_inc(turn_made, 1)

            pe.wait_ge(ident_in, 16)
            for slot, arrived in enumerate((ctx_in, wk_in)):
                pe.wait_ge(arrived, 16)
                for n in range(C * slot, C * slot + C):
                    turn(n, slot)
            pe.wait_ge(turn_lo, 2 * C)
            for j in range(C):
                for c in range(C):
                    for i, (left, right) in enumerate(PASSES):
                        last = pe.matmul(banks[j], turned[:, 1, left, c, P * j:P * j + P], turned[:, 0, right, c],
                                         start=(c == 0 and i == 0), stop=(c == C - 1 and i == 2))
                last.then_inc(key_made, 1)
            pe.wait_ge(wv_in, 16)
            for n in range(2 * C, 3 * C):
                turn(n, 2)
            pe.wait_ge(turn_lo, 3 * C)
            for r in range(C):
                pe.wait_ge(key_kept, r + 1)
                for c in range(C):
                    for i, (left, right) in enumerate(PASSES):
                        last = pe.matmul(banks[r], turned[:, 0, left, c, P * r:P * r + P], turned[:, 1, right, c],
                                         start=(c == 0 and i == 0), stop=(c == C - 1 and i == 2))
                last.then_inc(value_made, 1)
            pe.wait_ge(trig_neg, 1)
            for n in range(2 * C):
                quarter, imaginary = n // 2, n % 2
                if not imaginary:
                    pe.wait_ge(cols_lo, 2 * quarter + 2)
                if 4 <= n:
                    pe.wait_ge(value_kept, C)
                bank = banks[(4 + n) % 8]
                for parity in range(2):
                    products = [(which, table, c, left, right)
                                for which, table in enumerate((1, 2) if imaginary else (0, 1))
                                for c in range(2) for left, right in PASSES]
                    for i, (which, table, c, left, right) in enumerate(products):
                        last = pe.matmul(bank[:, HALF * parity:HALF * parity + HALF],
                                         columns[:, quarter % 2, which, left, parity, c],
                                         trig[:, table, right, parity, c],
                                         start=(i == 0), stop=(i == len(products) - 1))
                last.then_inc(g_made, 1)
            pe.wait_ge(g_lo, 2 * C)
            for n in range(C):
                for parity in range(2):
                    products = [(which, c, left, right) for c in range(2) for which in range(2) for left, right in PASSES]
                    for i, (which, c, left, right) in enumerate(products):
                        last = pe.matmul(banks[4 + n][:, HALF * parity:HALF * parity + HALF],
                                         spectra[:, which, left, 2 * parity + c, P * n:P * n + P],
                                         trig[:, which, right, parity, c],
                                         start=(i == 0), stop=(i == len(products) - 1))
                last.then_inc(a_made, 1)
            pe.wait_ge(a_sum, 2 * C)

            def step(b, k):
                if on(b, k):
                    if k == 0 and isinstance(b, int):
                        pe.wait_ge(keys_spread, 8)
                    due(pe, (q_lo, at(b, k // 2 * 2) + 2))
                    due(pe, (s_shifted, at(b, k)))
                    for j in range(C):
                        for i, (left, right) in enumerate(PASSES):
                            last = pe.matmul(ps_s[:, j // 2, 2 * P * (j % 2):2 * P * (j % 2) + 2 * P],
                                             q[:, (k // 2) % 2, left, j, P * (k % 2):P * (k % 2) + P],
                                             key_blocks[:, right, b + k // TPB if not isinstance(b, int) else k // TPB, j],
                                             start=(i == 0), stop=(i == 2))
                    last.then_inc(s_made, 1)
                if on(b, k - PAIR):
                    t = k - PAIR
                    if k == PAIR:
                        pe.wait_ge(weight_turned, 16)
                    due(pe, (n1_turned[t // 2 % 2], rounds(b, t // 2, TPB // 2) * 16 + 16))
                    due(pe, (q_kept, at(b, t)))
                    for i in range(2):
                        j = 2 * (t % 2) + i
                        for c in range(C):
                            for n, (left, right) in enumerate(PASSES):
                                last = pe.matmul(ps_q[:, i], WqT[:, left, j, c], n1T[:, (t // 2) % 2, right, :, c, :],
                                                 start=(c == 0 and n == 0), stop=(c == C - 1 and n == 2))
                    last.then_inc(q_made, 1)
                if on(b, k - VALUES):
                    t = k - VALUES
                    if t == 0 and isinstance(b, int):
                        pe.wait_ge(values_spread, 8)
                    due(pe, (p_turned[t % 2], rounds(b, t) * 16 + 16))
                    due(pe, (o_kept, at(b, t)))
                    batch = b + t // TPB if not isinstance(b, int) else t // TPB
                    for g in range(PAIRS):
                        for i, (left, right) in enumerate(PASSES):
                            width = VW if right == HIGH else 2 * HD
                            last = pe.matmul(ps_o[:, g, :width], probT[:, t % 2, left, g],
                                             value_blocks[:, right, batch, g, :width],
                                             start=(i == 0), stop=(i == 2))
                    last.then_inc(o_made, 1)
                if on(b, k - PROJECT):
                    t = k - PROJECT
                    if t == 0 and isinstance(b, int):
                        pe.wait_ge(weight_turned, 32)
                    due(pe, (o_turned[t % 2], rounds(b, t) * 16 + 16))
                    due(pe, (x2_made, at(b, t)))
                    for c in range(C):
                        for i, (left, right) in enumerate(PASSES):
                            last = pe.matmul(ps_proj[:], oT[:, t % 2, left, c], WoT[:, right, :, c, :],
                                             start=(c == 0 and i == 0), stop=(c == C - 1 and i == 2))
                    last.then_inc(proj_made, 1)
                if on(b, k - FORWARD):
                    t = k - FORWARD
                    if t == 0 and isinstance(b, int):
                        pe.wait_ge(ffn_lo, 1)
                    due(pe, (n2_turned[t % 2], rounds(b, t) * 16 + 16))
                    due(pe, (y_made, at(b, t)))
                    for c in range(C):
                        for i, (left, right) in enumerate(PASSES):
                            last = pe.matmul(ps_ffn[:], n2T[:, t % 2, left, c], ffn[:, right, c],
                                             start=(c == 0 and i == 0), stop=(c == C - 1 and i == 2))
                    last.then_inc(ffn_made, 1)

            steps(pe, step)


_INS = ["x", "ctx_1024", "L0_xattn_Wq", "L0_xattn_bq", "L0_xattn_Wk", "L0_xattn_bk", "L0_xattn_Wv", "L0_xattn_bv",
        "L0_xattn_Wo", "L0_xattn_bo", "L0_ffn_w_freq_real", "L0_ffn_w_freq_imag", "L0_ffn_bias"]


def kernel(**inputs):
    import numpy as _np
    import concourse.bacc as _bacc
    from concourse import mybir as _mybir
    from concourse.bass_utils import run_bass_kernel_spmd as _run

    nc = _bacc.Bacc("TRN2", target_bir_lowering=False, num_devices=1)
    arrays, args = {}, []

    def given(name, a):
        arrays[name] = a
        args.append(nc.dram_tensor(name, a.shape, _mybir.dt.from_np(a.dtype), kind="ExternalInput").ap())

    for name in _INS:
        given(f"in_{name}_dram", _np.ascontiguousarray(inputs[name]))
    width = inputs["x"].shape[-1]
    given("cos_sin_dram", _np.ascontiguousarray(tables(width).reshape(P, -1)))
    given("identity_dram", _np.eye(P, dtype=_np.float32))
    shape = inputs["x"].shape
    args.append(nc.dram_tensor("out_dram", shape, _mybir.dt.float32, kind="ExternalOutput").ap())
    xattn_ffn_kernel(nc, *args)
    r = _run(nc, [arrays], core_ids=[0])
    return r.results[0]["out_dram"]
```

```python
from contextlib import ExitStack

import numpy as np

import concourse.bass as bass
from concourse import mybir

F32 = mybir.dt.float32
F32R = mybir.dt.float32r
F16 = mybir.dt.float16
I32 = mybir.dt.int32
ALU = mybir.AluOpType
ACT = mybir.ActivationFunctionType
AX = mybir.AxisListType
RMAX = bass.bass_isa.ReduceOp.max

P = 128
EPS = 1e-5
HIGH, LOW = 0, 1
PASSES = ((HIGH, HIGH), (HIGH, LOW), (LOW, HIGH))
EXPONENT_BITS = 0x7F800000
LN_GAIN = 10
TOP = 13
P_GAIN = 14

LOAD, STORE = -8, 6


def tables(D):
    a = 2 * (P * np.arange(D // 2 // P)[None, None, :, None] + np.arange(P)[:, None, None, None]) \
        + np.arange(2)[None, :, None, None]
    angle = 2 * np.pi * ((a * np.arange(D // 2)) % D) / D
    return np.stack([np.cos(angle), np.sin(angle)], axis=1).astype(np.float32)


def xattn_ffn_kernel(nc, x, ctx, Wq, bq, Wk, bk, Wv, bv, Wo, bo, w_real, w_imag, bias, cos_sin, identity, out):
    B, S, D = x.shape
    KEYS = ctx.shape[1]
    HEADS = 16
    HD = D // HEADS
    C = D // P
    HALF = D // 2
    PAIRS = HEADS // 2
    HPC = P // HD
    TPB = S // P
    TILES = B * TPB
    TG = 2
    GROUPS = TPB // TG
    VW = 2 * HD + 2
    SCALE = 1.0 / float(np.sqrt(np.float32(HD)))
    assert TPB == 8 and C == 4 and KEYS * 2 == P and B * KEYS == D and B > 2

    x_groups = x.rearrange("b (g p t) f -> (b g) p t f", p=P, t=TG)
    out_groups = out.rearrange("b (g p t) f -> (b g) p t f", p=P, t=TG)

    stack = ExitStack()
    with stack:
        def sb(name, shape, dt, where=stack):
            return where.enter_context(nc.sbuf_tensor(name, shape, dt))

        def ps(name, shape):
            return stack.enter_context(nc.psum_tensor(name, shape, F32))

        def sem(name):
            return stack.enter_context(nc.semaphore(name))

        key_blocks = sb("key_blocks", [P, 2, B, C, HPC * KEYS], F16)
        value_blocks = sb("value_blocks", [P, 2, B, PAIRS, VW], F16)
        WqT = sb("WqT", [P, 2, C, C, P], F16)
        WoT = sb("WoT", [P, 2, C, C, P], F16)
        ffn = sb("ffn", [P, 2, C, D], F16)
        bo_rows = sb("bo_rows", [P, D], F32)
        bias_rows = sb("bias_rows", [P, D], F32)
        ident = sb("ident", [P, P], F32)
        bias_cols = sb("bias_cols", [P, 3, C], F32)
        peaks = sb("peaks", [P, 3, 8], F32)
        powers = sb("powers", [P, 8], F32)
        gains = sb("gains", [P, 3, 8], F32)
        factors = sb("factors", [P, 4], F32)
        minus_half = sb("minus_half", [P, 1], F32)
        wide = sb("wide", [P, C, D], F32)

        most = sb("most", [P, 2, HEADS], F32)
        per_sum = sb("per_sum", [P, 2, HEADS], F32)
        stats = sb("stats", [P, 2, 2, 6], F32)
        moments = sb("moments", [P, 2, 4, 2], F32)
        vareps = sb("vareps", [P, 2, 4], F32)
        rstd = sb("rstd", [P, 2, 4], F32)

        early = ExitStack()
        turned = sb("turned", [P, 2, 2, C, D], F32R, early)
        spectra = turned
        trig = sb("trig", [P, 3, 2, 2, 2, HALF], F32R, early)
        odd = sb("odd", [P, 2, HALF], F32, early)
        columns = sb("columns", [P, 2, 2, 2, 2, 2, P], F32R, early)
        sums = sb("sums", [P, 2, D], F32, early)
        parts = sb("parts", [P, 2, C, D], F16, early)
        kv_parts = ffn
        bv_rows = sb("bv_rows", [P, D], F32, early)
        keys = sb("keys", [P, C, D], F32, early)
        raw = sb("raw", [P, 3, C, D], F32, early)
        early.close()

        shifted = sb("shifted", [P, HEADS, KEYS], F32)
        prob = sb("prob", [P, HEADS * KEYS], F32)
        prob_parts = sb("prob_parts", [P, 2, 2, HEADS * KEYS], F16)
        probT = sb("probT", [P, 2, 2, PAIRS, P], F16)
        o_rows = sb("o_rows", [P, 2, D], F32)
        o_parts = sb("o_parts", [P, 2, 2, D], F16)
        oT = sb("oT", [P, 2, 2, C, P], F16)
        n2 = sb("n2", [P, 2, D], F32)
        n2_parts = sb("n2_parts", [P, 2, 2, D], F16)
        n2T = sb("n2T", [P, 2, 2, C, P], F16)
        q_sum = sb("q_sum", [P, 2, 2, 2 * P], F32)
        q = sb("q", [P, 2, 2, C, 2 * P], F16)
        n1T = sb("n1T", [P, 2, 2, 2, C, P], F16)
        n1 = sb("n1", [P, 2, D], F32)
        n1_parts = sb("n1_parts", [P, 2, 2, 2, D], F16)
        rows = sb("rows", [P, 2 * GROUPS, TG, D], F32)

        ps_q = ps("ps_q", [P, 2, 2 * P])
        ps_proj = ps("ps_proj", [P, D])
        ps_ffn = ps("ps_ffn", [P, D])
        ps_spare = ps("ps_spare", [P, D])
        ps_s = ps("ps_s", [P, 2, D])
        ps_o = ps("ps_o", [P, PAIRS, P])
        banks = [ps_q[:].rearrange("p a b -> p (a b)"),
                 ps_proj[:], ps_ffn[:], ps_spare[:], ps_s[:, 0, :], ps_s[:, 1, :],
                 ps_o[:, 0:4, :].rearrange("p a b -> p (a b)"), ps_o[:, 4:8, :].rearrange("p a b -> p (a b)")]

        ctx_in, wk_in, wv_in, trig_in, ident_in = map(sem, ("ctx_in", "wk_in", "wv_in", "trig_in", "ident_in"))
        real_in, imag_in, wq_in, wo_in = map(sem, ("real_in", "imag_in", "wq_in", "wo_in"))
        cols_in, bv_in, rows_in = map(sem, ("cols_in", "bv_in", "rows_in"))
        turn_made, key_made, value_made, g_made, a_made = map(sem, ("turn_made", "key_made", "value_made", "g_made", "a_made"))
        turn_hi, turn_lo, key_kept, value_kept = map(sem, ("turn_hi", "turn_lo", "key_kept", "value_kept"))
        trig_hi, trig_lo, trig_neg, cols_hi, cols_lo = map(sem, ("trig_hi", "trig_lo", "trig_neg", "cols_hi", "cols_lo"))
        g_odd, g_sum, g_hi, g_lo, a_odd, a_sum = map(sem, ("g_odd", "g_sum", "g_hi", "g_lo", "a_odd", "a_sum"))
        peak_own, peak_all, chain = map(sem, ("peak_own", "peak_all", "chain"))
        q_gain, k_gain, o_gain, v_gain, a_gain = map(sem, ("q_gain", "k_gain", "o_gain", "v_gain", "a_gain"))
        query_ready = sem("query_ready")
        part_hi, part_lo, kv_hi, kv_lo, weight_turned, keys_spread, values_spread = map(
            sem, ("part_hi", "part_lo", "kv_hi", "kv_lo", "weight_turned", "keys_spread", "values_spread"))
        filled, ones_set, ffn_hi, ffn_lo = map(sem, ("filled", "ones_set", "ffn_hi", "ffn_lo"))
        bn1, mv1, ve1, rs1, n1_made, n1_hi, n1_lo = map(sem, ("bn1", "mv1", "ve1", "rs1", "n1_made", "n1_hi", "n1_lo"))
        q_made, q_kept, q_hi, q_lo = map(sem, ("q_made", "q_kept", "q_hi", "q_lo"))
        s_made, s_max, s_shifted, p_made, p_hi, p_lo = map(
            sem, ("s_made", "s_max", "s_shifted", "p_made", "p_hi", "p_lo"))
        o_made, o_rec, o_kept, o_hi, o_lo = map(sem, ("o_made", "o_rec", "o_kept", "o_hi", "o_lo"))
        proj_made, xb_made, x2_made, bn2, mv2, ve2, rs2 = map(
            sem, ("proj_made", "xb_made", "x2_made", "bn2", "mv2", "ve2", "rs2"))
        n2_made, n2_hi, n2_lo, ffn_made, x2b_made, y_made = map(
            sem, ("n2_made", "n2_hi", "n2_lo", "ffn_made", "x2b_made", "y_made"))
        x_in, y_out = ([sem(f"{name}_{group}") for group in range(GROUPS)] for name in ("x_in", "y_out"))
        n1_turned, p_turned, o_turned, n2_turned = (
            [sem(f"{name}_{turn}") for turn in range(2)] for name in ("n1_turned", "p_turned", "o_turned", "n2_turned"))

        def due(eng, *waits, alone=False):
            waits = [(semaphore, value) for semaphore, value in waits if not isinstance(value, int) or value > 0]
            if alone and any(not isinstance(value, int) for _, value in waits):
                waits = [(semaphore, value if isinstance(value, int) else eng.to_reg(value)) for semaphore, value in waits]
                eng.wait_ge(waits[0][0], 1)
            for semaphore, value in waits:
                eng.wait_ge(semaphore, value)

        def steps(eng, step, after={}):
            for k in range(LOAD, TPB):
                step(0, k)
                if k in after:
                    after[k]()
            with eng.Fori(1, B - 1) as b:
                for k in range(TPB):
                    step(b, k)
            for k in range(TPB * (B - 1), TILES + STORE):
                step(0, k)

        def staged(*order):
            def step(b, k):
                for lag, stage in order:
                    if on(b, k - lag):
                        stage(b, k - lag)
            return step

        def on(b, k):
            return not isinstance(b, int) or 0 <= k < TILES

        def at(b, k):
            return b * TPB + k

        def slot_of(b, group):
            return ((b + group // GROUPS) % 2) * GROUPS + group % GROUPS

        def row_tile(b, k):
            return rows[:, slot_of(b, k // TG), k % TG, :]

        PQ, PB, PK, PV, PO, PA, PBIAS = range(7)
        SCORES, PROJ, FFN, QUERY = range(4)

        block = stack.enter_context(nc.Block())

        def rounds(b, t, each=TPB):
            return b * (each // 2) + t // 2

        @block.sync
        def _(sp):
            weight_rows = "(r p) f -> p r f"
            spectrum_rows = "(c p a) o -> a p c o"
            sp.dma_start(raw[:, 0], ctx.rearrange("b k f -> (b k) f").rearrange(weight_rows, p=P)).then_inc(ctx_in, 16)
            sp.dma_start(ident[:], identity).then_inc(ident_in, 16)
            sp.dma_start(raw[:, 1], Wk.rearrange(weight_rows, p=P)).then_inc(wk_in, 16)
            sp.dma_start(raw[:, 2], Wv.rearrange(weight_rows, p=P)).then_inc(wv_in, 16)
            sp.dma_start(wide[:].rearrange("p r n -> p (r n)"), cos_sin).then_inc(trig_in, 16)
            with nc.allow_non_contiguous_dma(reason="two biases as columns, 4 KB"):
                sp.dma_start(bias_cols[:, 0, :], bq.rearrange("(c p) -> p c", p=P)).then_inc(cols_in, 16)
                sp.dma_start(bias_cols[:, 1, :], bk.rearrange("(c p) -> p c", p=P)).then_inc(cols_in, 16)
            sp.wait_ge(turn_made, C)
            for a in range(2):
                sp.dma_start(raw[:, 0, 2 * a:2 * a + 2, :], w_real.rearrange(spectrum_rows, p=P, a=2)[a]).then_inc(real_in, 16)
            sp.wait_ge(turn_made, 2 * C)
            for a in range(2):
                sp.dma_start(raw[:, 1, 2 * a:2 * a + 2, :], w_imag.rearrange(spectrum_rows, p=P, a=2)[a]).then_inc(imag_in, 16)
            sp.wait_ge(turn_made, 3 * C)
            sp.dma_start(raw[:, 2], Wq.rearrange(weight_rows, p=P)).then_inc(wq_in, 16)
            sp.dma_start(bv_rows[:], bv.partition_broadcast(P)).then_inc(bv_in, 16)
            sp.dma_start(bo_rows[:], bo.partition_broadcast(P)).then_inc(rows_in, 16)
            sp.dma_start(bias_rows[:], bias.partition_broadcast(P)).then_inc(rows_in, 16)
            for n, turned_weight in enumerate((WqT, WoT)):
                sp.wait_ge(part_lo, n + 1)
                if n == 0:
                    sp.dma_start(raw[:, 2], Wo.rearrange(weight_rows, p=P)).then_inc(wo_in, 16)
                sp.dma_start_transpose(turned_weight[:].rearrange("p a r c o -> p (a r c) o"),
                                       parts[:].rearrange("p a r f -> p (a r f)")).then_inc(weight_turned, 16)
            sp.wait_ge(cols_lo, 8)
            sp.wait_ge(kv_lo, 1)
            sp.wait_ge(value_kept, C)
            sp.wait_ge(weight_turned, 32)

            def turn_n2(b, t):
                due(sp, (n2_lo, at(b, t) + 1),
                    (ffn_made, at(b, t) - 1), alone=True)
                sp.dma_start_transpose(n2T[:, t % 2].rearrange("p a c n -> p (a c) n"),
                                       n2_parts[:, t % 2].rearrange("p a f -> p (a f)")).then_inc(n2_turned[t % 2], 16)

            def store(b, t):
                if t % TG == TG - 1:
                    group = t // TG
                    due(sp, (y_made, at(b, t) + 1), alone=True)
                    sp.dma_start(out_groups[b * GROUPS + group], rows[:, slot_of(b, group)]).then_inc(y_out[group % GROUPS], 16)

            def load(b, t):
                if t % TG == 0:
                    group = t // TG
                    due(sp, (y_out[group % GROUPS], (b + group // GROUPS - 1) * 16), alone=True)
                    sp.dma_start(rows[:, slot_of(b, group)], x_groups[b * GROUPS + group]).then_inc(x_in[group % GROUPS], 16)

            def turn_n1(b, t):
                if t % 2 == 1:
                    ring = (t // 2) % 2
                    if t == 1 and isinstance(b, int):
                        sp.wait_ge(g_made, 2 * C)
                    due(sp, (n1_lo, at(b, t) + 1),
                        (q_made, at(b, t) - 3), alone=True)
                    sp.dma_start_transpose(n1T[:, ring].rearrange("p a t c n -> p (a t c) n"),
                                           n1_parts[:, ring].rearrange("p a t f -> p (a t f)")).then_inc(n1_turned[ring], 16)

            def turn_o(b, t):
                due(sp, (o_lo, at(b, t) + 1),
                    (proj_made, at(b, t) - 1), alone=True)
                sp.dma_start_transpose(oT[:, t % 2].rearrange("p a c n -> p (a c) n"),
                                       o_parts[:, t % 2].rearrange("p a f -> p (a f)")).then_inc(o_turned[t % 2], 16)

            def turn_p(b, t):
                due(sp, (p_lo, at(b, t) + 1),
                    (o_made, at(b, t) - 1), alone=True)
                sp.dma_start_transpose(probT[:, t % 2].rearrange("p a g n -> p (a g) n"),
                                       prob_parts[:, t % 2].rearrange("p a f -> p (a f)")).then_inc(p_turned[t % 2], 16)

            step = staged((5, turn_n2), (-8, load), (6, store), (-4, turn_n1), (2, turn_o), (0, turn_p))
            steps(sp, step)
            for done in y_out:
                sp.wait_ge(done, B * 16)

        @block.gpsimd
        def _(pool):
            pool.memset(minus_half[:], -0.5).then_inc(filled, 1)
            pool.memset(value_blocks[:].rearrange("p a b g w -> p (a b g w)").bitcast(F32), 0.0).then_inc(filled, 1)
            pool.memset(key_blocks[:].rearrange("p a b c w -> p (a b c w)").bitcast(F32), 0.0).then_inc(filled, 1)
            pool.wait_ge(filled, 3)
            for head in range(2):
                rows_of = slice(head * KEYS, head * KEYS + KEYS)
                pool.memset(value_blocks[rows_of, HIGH, :, :, 2 * HD + head:2 * HD + head + 1], 1.0).then_inc(ones_set, 1)
            pool.wait_ge(ones_set, 2)

            peaks_seen = [0]

            def peak_of_all(col):
                peaks_seen[0] += 1
                pool.wait_ge(peak_own, peaks_seen[0])
                pool.partition_all_reduce(peaks[:, 1, col:col + 1], peaks[:, 0, col:col + 1], P, RMAX).then_inc(peak_all, 1)

            def rest(to, whole, high):
                return pool.tensor_tensor(to, whole, high, ALU.subtract)

            def columns_rest(n):
                for which in range(2):
                    pool.wait_ge(cols_hi, 2 * n + which + 1)
                    rest(columns[:, n % 2, which, LOW].rearrange("p a c o -> p (a c) o"),
                         raw[:, which].rearrange("p r (o a) -> p r o a", a=2)[:, :, P * (n % 2):P * (n % 2) + P, n // 2],
                         columns[:, n % 2, which, HIGH].rearrange("p a c o -> p (a c) o").bitcast(F32)).then_inc(cols_lo, 1)

            def spectrum_rest(n):
                pool.wait_ge(g_hi, n + 1)
                rest(spectra[:, n % 2, LOW, n // 2], sums[:, n % 2],
                     spectra[:, n % 2, HIGH, n // 2].bitcast(F32)).then_inc(g_lo, 1)

            peak_of_all(PBIAS)
            columns_rest(0)
            peak_of_all(PQ)
            columns_rest(1)
            peak_of_all(PK)
            columns_rest(2)
            peak_of_all(PO)
            spectrum_rest(0)
            spectrum_rest(1)
            peak_of_all(PV)
            spectrum_rest(2)
            columns_rest(3)
            for n in range(3, 2 * C):
                spectrum_rest(n)

            def deviation(b, t, moments_made, sum_made, done, norm):
                slot = slice(t % 4, t % 4 + 1)
                due(pool, (moments_made, at(b, t) + 1), alone=True)
                pool.tensor_scalar(vareps[:, norm, slot], moments[:, norm, t % 4, 1:2], EPS, 2.0 ** (-2 * LN_GAIN),
                                   ALU.add, ALU.mult).then_inc(sum_made, 1)
                due(pool, (sum_made, at(b, t) + 1), alone=True)
                pool.tensor_tensor(rstd[:, norm, slot], vareps[:, norm, slot], minus_half[:], ALU.pow).then_inc(done, 1)

            def n2_rest(b, t):
                due(pool, (n2_hi, at(b, t) + 1), alone=True)
                rest(n2_parts[:, t % 2, LOW], n2[:, t % 2], n2_parts[:, t % 2, HIGH]).then_inc(n2_lo, 1)

            def deviation1(b, t):
                deviation(b, t, mv1, ve1, rs1, 0)

            def deviation2(b, t):
                deviation(b, t, mv2, ve2, rs2, 1)

            def add_bias(b, t):
                due(pool, (n2_made, at(b, t) + 1), alone=True)
                row = row_tile(b, t)
                pool.tensor_tensor(row, row, bias_rows[:], ALU.add).then_inc(x2b_made, 1)

            def n1_rest(b, t):
                due(pool, (n1_hi, at(b, t) + 1), alone=True)
                rest(n1_parts[:, (t // 2) % 2, LOW, t % 2], n1[:, t % 2],
                     n1_parts[:, (t // 2) % 2, HIGH, t % 2]).then_inc(n1_lo, 1)

            def add_bo(b, t):
                if t == 0 and isinstance(b, int):
                    pool.wait_ge(rows_in, 32)
                due(pool, (n1_made, at(b, t) + 1), alone=True)
                row = row_tile(b, t)
                pool.tensor_tensor(row, row, bo_rows[:], ALU.add).then_inc(xb_made, 1)

            def q_rest(b, t):
                due(pool, (q_hi, at(b, t) + 1), alone=True)
                half = slice(2 * (t % 2), 2 * (t % 2) + 2)
                rest(q[:, (t // 2) % 2, LOW, half], q_sum[:, t % 2], q[:, (t // 2) % 2, HIGH, half]).then_inc(q_lo, 1)

            step = staged((4, deviation2), (5, add_bias), (-4, n1_rest), (-2, q_rest), (-4, add_bo), (-6, deviation1),
                          (4, n2_rest))
            steps(pool, step, {-1: lambda: peak_of_all(PA)})

        @block.scalar
        def _(act):
            def high(to, whole, col=None):
                if col is None:
                    return act.activation(to, whole, ACT.Copy)
                return act.activation(to, whole, ACT.Identity, bias=0.0, scale=gains[:, 1, col:col + 1])

            def turn(n):
                act.wait_ge(turn_made, n + 1)
                high(turned[:, min(n // C, 1), HIGH, n % C], banks[n % 8 if n < 8 else 4 + n % C]).then_inc(turn_hi, 1)

            def column_parts(n):
                if n == 0:
                    act.wait_ge(real_in, 32)
                    act.wait_ge(imag_in, 32)
                if n >= 2:
                    act.wait_ge(g_made, 2 * n - 2)
                for which in range(2):
                    high(columns[:, n % 2, which, HIGH].rearrange("p a c o -> p (a c) o"),
                         raw[:, which].rearrange("p r (o a) -> p r o a", a=2)[:, :, P * (n % 2):P * (n % 2) + P, n // 2]
                         ).then_inc(cols_hi, 1)

            def spectrum_odd(n):
                act.wait_ge(g_made, n + 1)
                if n >= 2:
                    act.wait_ge(g_sum, 2 * n - 2)
                act.activation(odd[:, n % 2], banks[n][:, HALF:], ACT.Copy).then_inc(g_odd, 1)

            def spectrum_high(n):
                act.wait_ge(g_sum, 2 * n + 2)
                if n == 0:
                    act.wait_ge(value_made, C)
                high(spectra[:, n % 2, HIGH, n // 2], sums[:, n % 2]).then_inc(g_hi, 1)

            def split(to, whole, col, ready, done):
                act.wait_ge(ready, 1)
                high(to[:, HIGH], whole, col).then_inc(done, 1)

            def take_key(j):
                act.wait_ge(key_made, j + 1)
                act.activation(keys[:, j], banks[j], ACT.Identity, bias=bias_cols[:, 1, j:j + 1]).then_inc(key_kept, 1)

            def minus_cos(part, ready):
                act.wait_ge(ready, 1)
                act.mul(trig_flat[:, 2, part], trig_flat[:, 0, part].bitcast(F32), -1.0).then_inc(trig_neg, 1)

            for n in range(2 * C):
                turn(n)
            act.wait_ge(trig_in, 16)
            tables_in = wide[:].rearrange("p (t r) n -> p t (r n)", t=2)
            trig_flat = trig[:].rearrange("p t s a c n -> p t s (a c n)")
            high(trig_flat[:, 0:2, HIGH], tables_in).then_inc(trig_hi, 1)
            act.wait_ge(cols_in, 32)
            take_key(0)
            minus_cos(HIGH, trig_hi)
            take_key(1)
            minus_cos(LOW, trig_lo)
            column_parts(0)
            take_key(2)
            take_key(3)
            for n in range(2 * C, 3 * C):
                turn(n)
            column_parts(1)
            split(parts, raw[:, 2], PQ, q_gain, part_hi)
            spectrum_odd(0)
            spectrum_odd(1)
            column_parts(2)
            split(kv_parts, keys[:], PK, k_gain, kv_hi)
            act.wait_ge(weight_turned, 16)
            split(parts, raw[:, 2], PO, o_gain, part_hi)
            spectrum_high(0)
            spectrum_high(1)
            spectrum_odd(2)
            spectrum_high(2)
            spectrum_odd(3)
            column_parts(3)
            spectrum_high(3)
            act.wait_ge(keys_spread, 8)
            split(kv_parts, wide[:], PV, v_gain, kv_hi)
            for n in range(4, 2 * C):
                spectrum_odd(n)
                spectrum_high(n)

            def matrix(n):
                act.wait_ge(a_made, n + 1)
                if n >= 2:
                    act.wait_ge(a_sum, 2 * n - 2)
                act.activation(odd[:, n % 2], banks[n][:, HALF:], ACT.Copy).then_inc(a_odd, 1)

            def n2_high(b, t):
                due(act, (n2_made, at(b, t) + 1))
                due(act, (n2_turned[t % 2], rounds(b, t) * 16))
                high(n2_parts[:, t % 2, HIGH], n2[:, t % 2]).then_inc(n2_hi, 1)

            def n1_high(b, t):
                if t == 0 and isinstance(b, int):
                    act.wait_ge(g_lo, 2 * C)
                due(act, (n1_made, at(b, t) + 1))
                due(act, (n1_turned[t // 2 % 2], rounds(b, t // 2, TPB // 2) * 16))
                high(n1_parts[:, (t // 2) % 2, HIGH, t % 2], n1[:, t % 2]).then_inc(n1_hi, 1)

            def exponentials(b, t):
                if t == 0 and isinstance(b, int):
                    act.wait_ge(query_ready, 2)
                due(act, (s_shifted, at(b, t) + 1))
                due(act, (p_lo, at(b, t)))
                act.activation(prob[:], shifted[:].rearrange("p h n -> p (h n)"), ACT.Exp,
                               scale=factors[:, SCORES:SCORES + 1]).then_inc(p_made, 1)

            def p_high(b, t):
                due(act, (p_made, at(b, t) + 1))
                due(act, (p_turned[t % 2], rounds(b, t) * 16))
                act.activation(prob_parts[:, t % 2, HIGH], prob[:], ACT.Copy, scale=2.0 ** P_GAIN).then_inc(p_hi, 1)

            def take_q(b, t):
                if t == 0 and isinstance(b, int):
                    act.wait_ge(query_ready, 2)
                due(act, (q_made, at(b, t) + 1))
                due(act, (q_lo, at(b, t) - 1))
                for i in range(2):
                    j = 2 * (t % 2) + i
                    last = act.activation(q_sum[:, t % 2, i], ps_q[:, i], ACT.Identity,
                                          bias=bias_cols[:, 2, j:j + 1], scale=factors[:, QUERY:QUERY + 1])
                last.then_inc(q_kept, 1)

            def q_high(b, t):
                if t == 0 and isinstance(b, int):
                    act.wait_ge(a_sum, 2 * C)
                due(act, (q_kept, at(b, t) + 1))
                due(act, (s_made, at(b, t // 2 * 2) - 2))
                high(q[:, (t // 2) % 2, HIGH, 2 * (t % 2):2 * (t % 2) + 2], q_sum[:, t % 2]).then_inc(q_hi, 1)

            def o_high(b, t):
                due(act, (o_kept, at(b, t) + 1))
                due(act, (o_turned[t % 2], rounds(b, t) * 16))
                high(o_parts[:, t % 2, HIGH], o_rows[:, t % 2]).then_inc(o_hi, 1)

            step = staged((5, n2_high), (0, exponentials), (0, p_high), (-2, take_q), (-2, q_high), (2, o_high),
                          (-5, n1_high))

            def matrices():
                for n in range(C):
                    matrix(n)

            def matrix_high():
                act.wait_ge(values_spread, 8)
                split(ffn, wide[:], PA, a_gain, ffn_hi)

            steps(act, step, {-3: matrices, 1: matrix_high})

        @block.vector
        def _(dve):
            links = [0]

            def link(instruction):
                links[0] += 1
                instruction.then_inc(chain, 1)
                dve.wait_ge(chain, links[0])

            def rest(to, whole, high):
                return dve.tensor_tensor(to, whole, high, ALU.subtract)

            def turn(n):
                dve.wait_ge(turn_hi, n + 1)
                rest(turned[:, min(n // C, 1), LOW, n % C], banks[n % 8 if n < 8 else 4 + n % C],
                     turned[:, min(n // C, 1), HIGH, n % C].bitcast(F32)).then_inc(turn_lo, 1)

            def own_peak(col, whole):
                dve.tensor_reduce(peaks[:, 0, col:col + 1], whole, AX.X, ALU.max,
                                  apply_absolute_value=True).then_inc(peak_own, 1)

            def power(col, number, clipped=False):
                if not clipped:
                    dve.wait_ge(peak_all, number)
                    link(dve.tensor_scalar(peaks[:, 2, col:col + 1], peaks[:, 1, col:col + 1], 1e-30, None, ALU.max))
                link(dve.tensor_scalar(powers[:, col:col + 1].bitcast(I32), peaks[:, 2, col:col + 1].bitcast(I32),
                                       EXPONENT_BITS, None, ALU.bitwise_and))
                link(dve.reciprocal(gains[:, 0, col:col + 1], powers[:, col:col + 1]))

            def gain(col, ready):
                dve.tensor_scalar(gains[:, 1, col:col + 1], gains[:, 0, col:col + 1], 2.0 ** TOP, None,
                                  ALU.mult).then_inc(ready, 1)

            def split_rest(n, to, whole, high, col, hi_done, lo_done):
                dve.wait_ge(hi_done, n + 1)
                dve.scalar_tensor_tensor(out=to, in0=whole, scalar=gains[:, 1, col:col + 1], in1=high,
                                         op0=ALU.mult, op1=ALU.subtract).then_inc(lo_done, 1)

            def spread_keys():
                dve.wait_ge(filled, 3)
                dve.wait_ge(kv_lo, 1)
                for part in range(2):
                    for h in range(HPC):
                        of = slice(HD * h, HD * h + HD)
                        dve.tensor_copy(key_blocks[of, part, :, :, KEYS * h:KEYS * h + KEYS],
                                        kv_parts[of, part].rearrange("p c (b n) -> p b c n", b=B)).then_inc(keys_spread, 1)

            def spread_values():
                dve.wait_ge(ones_set, 2)
                dve.wait_ge(kv_lo, 2)
                for part in range(2):
                    for b in range(2):
                        for h in range(2):
                            dve.tensor_copy(
                                value_blocks[KEYS * h:KEYS * h + KEYS, part, b::2, :, HD * h:HD * h + HD],
                                kv_parts[KEYS * b:KEYS * b + KEYS, part].rearrange("p r (g h d) -> p r g h d", h=2, d=HD)[:, :, :, h]
                            ).then_inc(values_spread, 1)

            def take_value(r):
                if r == 0:
                    dve.wait_ge(bv_in, 16)
                    dve.wait_ge(trig_lo, 1)
                dve.wait_ge(value_made, r + 1)
                dve.tensor_tensor(wide[:, r], banks[4 + r], bv_rows[:], ALU.add).then_inc(value_kept, 1)

            def spectrum(n):
                dve.wait_ge(g_odd, n + 1)
                if n >= 2:
                    dve.wait_ge(g_lo, n - 1)
                for half, op in enumerate((ALU.add, ALU.subtract)):
                    dve.tensor_tensor(sums[:, n % 2, HALF * half:HALF * half + HALF], banks[n][:, :HALF], odd[:, n % 2],
                                      op).then_inc(g_sum, 1)

            for n in range(2 * C):
                turn(n)
            dve.wait_ge(trig_hi, 1)
            tables_in = wide[:].rearrange("p (t r) n -> p t (r n)", t=2)
            trig_flat = trig[:].rearrange("p t s a c n -> p t s (a c n)")
            rest(trig_flat[:, 0:2, LOW], tables_in, trig_flat[:, 0:2, HIGH].bitcast(F32)).then_inc(trig_lo, 1)
            dve.wait_ge(cols_in, 32)
            own_peak(PBIAS, bias_cols[:, 0, :])
            dve.wait_ge(wq_in, 16)
            own_peak(PQ, raw[:, 2].rearrange("p c n -> p (c n)"))
            for n in range(2 * C, 3 * C):
                turn(n)
            power(PBIAS, 1)
            power(PQ, 2)
            gain(PQ, q_gain)
            dve.wait_ge(key_kept, C)
            own_peak(PK, keys[:].rearrange("p c n -> p (c n)"))
            link(dve.scalar_tensor_tensor(out=peaks[:, 2, PB:PB + 1], in0=peaks[:, 2, PQ:PQ + 1], scalar=float(D),
                                          in1=peaks[:, 2, PBIAS:PBIAS + 1], op0=ALU.mult, op1=ALU.add))
            power(PB, 0, clipped=True)
            link(dve.tensor_scalar(gains[:, 1, PB:PB + 1], gains[:, 0, PB:PB + 1], 2.0 ** (TOP + 1), None, ALU.mult))
            dve.tensor_scalar(bias_cols[:, 2, :], bias_cols[:, 0, :], gains[:, 1, PB:PB + 1], None, ALU.mult)
            dve.tensor_scalar(factors[:, QUERY:QUERY + 1], powers[:, PQ:PQ + 1], gains[:, 1, PB:PB + 1],
                              2.0 ** -(TOP + LN_GAIN), ALU.mult, ALU.mult).then_inc(query_ready, 1)
            split_rest(0, parts[:, LOW], raw[:, 2], parts[:, HIGH], PQ, part_hi, part_lo)
            spectrum(0)
            power(PK, 3)
            gain(PK, k_gain)
            dve.tensor_scalar(factors[:, SCORES:SCORES + 1], powers[:, PB:PB + 1], powers[:, PK:PK + 1],
                              SCALE * 2.0 ** -(2 * TOP + 1), ALU.mult, ALU.mult).then_inc(query_ready, 1)
            spectrum(1)
            take_value(0)
            dve.wait_ge(wo_in, 16)
            own_peak(PO, raw[:, 2].rearrange("p c n -> p (c n)"))
            take_value(1)
            split_rest(0, kv_parts[:, LOW], keys[:], kv_parts[:, HIGH], PK, kv_hi, kv_lo)
            take_value(2)
            power(PO, 4)
            gain(PO, o_gain)
            spread_keys()
            take_value(3)
            dve.wait_ge(value_kept, C)
            own_peak(PV, wide[:].rearrange("p c n -> p (c n)"))
            split_rest(1, parts[:, LOW], raw[:, 2], parts[:, HIGH], PO, part_hi, part_lo)
            spectrum(2)
            power(PV, 5)
            gain(PV, v_gain)
            link(dve.tensor_scalar(factors[:, PROJ:PROJ + 1], powers[:, PV:PV + 1], powers[:, PO:PO + 1],
                                   2.0 ** -(2 * TOP), ALU.mult, ALU.mult))
            spectrum(3)
            split_rest(1, kv_parts[:, LOW], wide[:], kv_parts[:, HIGH], PV, kv_hi, kv_lo)
            spectrum(4)
            spread_values()
            for n in range(5, 2 * C):
                spectrum(n)

            def normal(to, row, t, norm):
                return dve.tensor_scalar(to, row, moments[:, norm, t % 4, 0:1], rstd[:, norm, t % 4:t % 4 + 1],
                                         ALU.subtract, ALU.mult)

            def result(b, t):
                row = row_tile(b, t)
                due(dve, (ffn_made, at(b, t) + 1))
                due(dve, (x2b_made, at(b, t) + 1))
                dve.scalar_tensor_tensor(out=row, in0=ps_ffn[:], scalar=factors[:, FFN:FFN + 1], in1=row,
                                         op0=ALU.mult, op1=ALU.add).then_inc(y_made, 1)

            def second_norm(b, t):
                due(dve, (rs2, at(b, t) + 1))
                due(dve, (n2_lo, at(b, t) - 1))
                normal(n2[:, t % 2], row_tile(b, t), t, 1).then_inc(n2_made, 1)

            def first_norm(b, t):
                if t == 0 and isinstance(b, int):
                    dve.wait_ge(g_made, 2 * C)
                due(dve, (rs1, at(b, t) + 1))
                due(dve, (n1_lo, at(b, t) - 1))
                normal(n1[:, t % 2], row_tile(b, t), t, 0).then_inc(n1_made, 1)

            def maximum(b, t):
                due(dve, (s_made, at(b, t) + 1))
                scores = ps_s[:].rearrange("p a (h n) -> p (a h) n", n=KEYS)
                dve.tensor_reduce(most[:, t % 2], scores, AX.X, ALU.max).then_inc(s_max, 1)

            def shift(b, t):
                scores = ps_s[:].rearrange("p a (h n) -> p (a h) n", n=KEYS)
                due(dve, (s_max, at(b, t) + 1))
                due(dve, (p_made, at(b, t)))
                dve.tensor_tensor(shifted[:], scores, most[:, t % 2].unsqueeze(2).to_broadcast([P, HEADS, KEYS]),
                                  ALU.subtract).then_inc(s_shifted, 1)

            def stat1(b, t):
                if t % TG == 0:
                    due(dve, (x_in[t // TG % GROUPS], (b + t // TG // GROUPS + 1) * 16), alone=True)
                dve.bn_stats(stats[:, 0, t % 2], row_tile(b, t)).then_inc(bn1, 1)

            def moments1(b, t):
                due(dve, (bn1, at(b, t) + 1), alone=True)
                dve.bn_aggr(moments[:, 0, t % 4], stats[:, 0, t % 2]).then_inc(mv1, 1)

            def reciprocals(b, t):
                due(dve, (o_made, at(b, t) + 1))
                dve.reciprocal(per_sum[:, t % 2].rearrange("p (g h) -> p g h", h=2),
                               ps_o[:, :, 2 * HD:VW]).then_inc(o_rec, 1)

            def take_o(b, t):
                due(dve, (o_rec, at(b, t) + 1))
                due(dve, (o_lo, at(b, t) - 1))
                dve.tensor_tensor(
                    o_rows[:, t % 2].rearrange("p (g h d) -> p g h d", h=2, d=HD),
                    ps_o[:, :, 0:2 * HD].rearrange("p g (h d) -> p g h d", h=2),
                    per_sum[:, t % 2].rearrange("p (g h) -> p g h", h=2).unsqueeze(3).to_broadcast([P, PAIRS, 2, HD]),
                    ALU.mult).then_inc(o_kept, 1)

            def p_rest(b, t):
                due(dve, (p_hi, at(b, t) + 1))
                dve.scalar_tensor_tensor(out=prob_parts[:, t % 2, LOW], in0=prob[:], scalar=2.0 ** P_GAIN,
                                         in1=prob_parts[:, t % 2, HIGH], op0=ALU.mult,
                                         op1=ALU.subtract).then_inc(p_lo, 1)

            def o_rest(b, t):
                due(dve, (o_hi, at(b, t) + 1))
                rest(o_parts[:, t % 2, LOW], o_rows[:, t % 2], o_parts[:, t % 2, HIGH]).then_inc(o_lo, 1)

            def residual(b, t):
                row = row_tile(b, t)
                due(dve, (proj_made, at(b, t) + 1))
                due(dve, (xb_made, at(b, t) + 1))
                dve.scalar_tensor_tensor(out=row, in0=ps_proj[:], scalar=factors[:, PROJ:PROJ + 1], in1=row,
                                         op0=ALU.mult, op1=ALU.add).then_inc(x2_made, 1)

            def stat2(b, t):
                due(dve, (x2_made, at(b, t) + 1), alone=True)
                dve.bn_stats(stats[:, 1, t % 2], row_tile(b, t)).then_inc(bn2, 1)

            def moments2(b, t):
                due(dve, (bn2, at(b, t) + 1), alone=True)
                dve.bn_aggr(moments[:, 1, t % 4], stats[:, 1, t % 2]).then_inc(mv2, 1)

            step = staged((4, moments2), (0, maximum), (0, shift), (4, second_norm), (6, result), (-6, stat1),
                          (-6, moments1), (-5, first_norm), (2, reciprocals), (2, take_o), (0, p_rest), (3, residual),
                          (2, o_rest), (3, stat2))

            def matrices():
                for n in range(C):
                    dve.wait_ge(a_odd, n + 1)
                    for half, op in enumerate((ALU.add, ALU.subtract)):
                        dve.tensor_tensor(wide[:, n, HALF * half:HALF * half + HALF], banks[n][:, :HALF], odd[:, n % 2],
                                          op).then_inc(a_sum, 1)

            def matrix_peak():
                dve.wait_ge(a_sum, 2 * C)
                own_peak(PA, wide[:].rearrange("p c n -> p (c n)"))

            def matrix_gain():
                power(PA, 6)
                gain(PA, a_gain)
                link(dve.tensor_scalar(factors[:, FFN:FFN + 1], powers[:, PA:PA + 1], 2.0 ** -(TOP + LN_GAIN) / D, None,
                                       ALU.mult))

            def matrix_rest():
                split_rest(0, ffn[:, LOW], wide[:], ffn[:, HIGH], PA, ffn_hi, ffn_lo)

            steps(dve, step, {-3: matrices, -2: matrix_peak, 0: matrix_gain, 2: matrix_rest})

        @block.tensor
        def _(pe):
            def turn(n, slot):
                for r in range(C):
                    last = pe.transpose(banks[n if n < 2 * C else n - C][:, P * r:P * r + P],
                                        raw[:, slot, r, P * (n % C):P * (n % C) + P], ident[:])
                last.then_inc(turn_made, 1)

            pe.wait_ge(ident_in, 16)
            for slot, arrived in enumerate((ctx_in, wk_in, wv_in)):
                pe.wait_ge(arrived, 16)
                for n in range(C * slot, C * slot + C):
                    if slot == 2:
                        pe.wait_ge(turn_lo, n - C + 1)
                    turn(n, slot)
            for j in range(C):
                for c in range(C):
                    for i, (left, right) in enumerate(PASSES):
                        last = pe.matmul(banks[j], turned[:, 1, left, c, P * j:P * j + P], turned[:, 0, right, c],
                                         start=(c == 0 and i == 0), stop=(c == C - 1 and i == 2))
                last.then_inc(key_made, 1)

            def spectrum(n):
                quarter, imaginary = n // 2, n % 2
                if not imaginary:
                    pe.wait_ge(cols_lo, 2 * quarter + 2)
                for parity in range(2):
                    products = [(which, table, c, left, right)
                                for which, table in enumerate((1, 2) if imaginary else (0, 1))
                                for c in range(2) for left, right in PASSES]
                    for i, (which, table, c, left, right) in enumerate(products):
                        last = pe.matmul(banks[n][:, HALF * parity:HALF * parity + HALF],
                                         columns[:, quarter % 2, which, left, parity, c],
                                         trig[:, table, right, parity, c],
                                         start=(i == 0), stop=(i == len(products) - 1))
                last.then_inc(g_made, 1)

            pe.wait_ge(trig_neg, 2)
            pe.wait_ge(key_kept, 2)
            spectrum(0)
            spectrum(1)
            pe.wait_ge(turn_lo, 3 * C)
            for r in range(C):
                for c in range(C):
                    for i, (left, right) in enumerate(PASSES):
                        last = pe.matmul(banks[4 + r], turned[:, 0, left, c, P * r:P * r + P], turned[:, 1, right, c],
                                         start=(c == 0 and i == 0), stop=(c == C - 1 and i == 2))
                last.then_inc(value_made, 1)
            pe.wait_ge(key_kept, C)
            spectrum(2)
            spectrum(3)
            pe.wait_ge(value_kept, C)
            for n in range(4, 2 * C):
                spectrum(n)
            for parity in range(2):
                pe.wait_ge(g_lo, C * parity + C)
                for n in range(C):
                    products = [(which, c, left, right) for c in range(2) for which in range(2) for left, right in PASSES]
                    for i, (which, c, left, right) in enumerate(products):
                        last = pe.matmul(banks[n][:, HALF * parity:HALF * parity + HALF],
                                         spectra[:, which, left, 2 * parity + c, P * n:P * n + P],
                                         trig[:, which, right, parity, c],
                                         start=(i == 0), stop=(i == len(products) - 1))
                    if parity == 1:
                        last.then_inc(a_made, 1)

            def scores(b, t):
                if t == 0 and isinstance(b, int):
                    pe.wait_ge(keys_spread, 8)
                due(pe, (q_lo, at(b, t // 2 * 2) + 2))
                due(pe, (s_shifted, at(b, t)))
                for j in range(C):
                    for i, (left, right) in enumerate(PASSES):
                        last = pe.matmul(ps_s[:, j // 2, 2 * P * (j % 2):2 * P * (j % 2) + 2 * P],
                                         q[:, (t // 2) % 2, left, j, P * (t % 2):P * (t % 2) + P],
                                         key_blocks[:, right, b + t // TPB, j], start=(i == 0), stop=(i == 2))
                last.then_inc(s_made, 1)

            def queries(b, t):
                if t == 0 and isinstance(b, int):
                    pe.wait_ge(weight_turned, 16)
                    pe.wait_ge(a_sum, 2)
                due(pe, (n1_turned[t // 2 % 2], rounds(b, t // 2, TPB // 2) * 16 + 16))
                due(pe, (q_kept, at(b, t)))
                for i in range(2):
                    j = 2 * (t % 2) + i
                    for c in range(C):
                        for n, (left, right) in enumerate(PASSES):
                            last = pe.matmul(ps_q[:, i], WqT[:, left, j, c], n1T[:, (t // 2) % 2, right, :, c, :],
                                             start=(c == 0 and n == 0), stop=(c == C - 1 and n == 2))
                last.then_inc(q_made, 1)

            def values(b, t):
                if t == 0 and isinstance(b, int):
                    pe.wait_ge(values_spread, 8)
                due(pe, (p_turned[t % 2], rounds(b, t) * 16 + 16))
                due(pe, (o_kept, at(b, t)))
                for g in range(PAIRS):
                    for i, (left, right) in enumerate(PASSES):
                        width = VW if right == HIGH else 2 * HD
                        last = pe.matmul(ps_o[:, g, :width], probT[:, t % 2, left, g],
                                         value_blocks[:, right, b + t // TPB, g, :width], start=(i == 0), stop=(i == 2))
                last.then_inc(o_made, 1)

            def project(b, t):
                if t == 0 and isinstance(b, int):
                    pe.wait_ge(weight_turned, 32)
                    pe.wait_ge(a_sum, 2 * C)
                due(pe, (o_turned[t % 2], rounds(b, t) * 16 + 16))
                due(pe, (x2_made, at(b, t)))
                for c in range(C):
                    for i, (left, right) in enumerate(PASSES):
                        last = pe.matmul(ps_proj[:], oT[:, t % 2, left, c], WoT[:, right, :, c, :],
                                         start=(c == 0 and i == 0), stop=(c == C - 1 and i == 2))
                last.then_inc(proj_made, 1)

            def forward(b, t):
                if t == 0 and isinstance(b, int):
                    pe.wait_ge(ffn_lo, 1)
                due(pe, (n2_turned[t % 2], rounds(b, t) * 16 + 16))
                due(pe, (y_made, at(b, t)))
                for c in range(C):
                    for i, (left, right) in enumerate(PASSES):
                        last = pe.matmul(ps_ffn[:], n2T[:, t % 2, left, c], ffn[:, right, c],
                                         start=(c == 0 and i == 0), stop=(c == C - 1 and i == 2))
                last.then_inc(ffn_made, 1)

            step = staged((0, scores), (-2, queries), (2, values), (3, project), (5, forward))
            steps(pe, step)


_INS = ["x", "ctx_1024", "L0_xattn_Wq", "L0_xattn_bq", "L0_xattn_Wk", "L0_xattn_bk", "L0_xattn_Wv", "L0_xattn_bv",
        "L0_xattn_Wo", "L0_xattn_bo", "L0_ffn_w_freq_real", "L0_ffn_w_freq_imag", "L0_ffn_bias"]


def kernel(**inputs):
    import numpy as _np
    import concourse.bacc as _bacc
    from concourse import mybir as _mybir
    from concourse.bass_utils import run_bass_kernel_spmd as _run

    nc = _bacc.Bacc("TRN2", target_bir_lowering=False, num_devices=1)
    arrays, args = {}, []

    def given(name, a):
        arrays[name] = a
        args.append(nc.dram_tensor(name, a.shape, _mybir.dt.from_np(a.dtype), kind="ExternalInput").ap())

    for name in _INS:
        given(f"in_{name}_dram", _np.ascontiguousarray(inputs[name]))
    width = inputs["x"].shape[-1]
    given("cos_sin_dram", _np.ascontiguousarray(tables(width).reshape(P, -1)))
    given("identity_dram", _np.eye(P, dtype=_np.float32))
    shape = inputs["x"].shape
    args.append(nc.dram_tensor("out_dram", shape, _mybir.dt.float32, kind="ExternalOutput").ap())
    xattn_ffn_kernel(nc, *args)
    r = _run(nc, [arrays], core_ids=[0])
    return r.results[0]["out_dram"]
```

```python
from contextlib import ExitStack

import numpy as np

import concourse.bass as bass
from concourse import mybir

F32 = mybir.dt.float32
F32R = mybir.dt.float32r
F16 = mybir.dt.float16
I32 = mybir.dt.int32
ALU = mybir.AluOpType
ACT = mybir.ActivationFunctionType
AX = mybir.AxisListType
RMAX = bass.bass_isa.ReduceOp.max

P = 128
EPS = 1e-5
HIGH, LOW = 0, 1
PASSES = ((HIGH, HIGH), (HIGH, LOW), (LOW, HIGH))
EXPONENT_BITS = 0x7F800000
LN_GAIN = 10
TOP = 13
P_GAIN = 14

LOAD, STORE = -8, 8


def tables(D):
    a = 2 * (P * np.arange(D // 2 // P)[None, None, :, None] + np.arange(P)[:, None, None, None]) \
        + np.arange(2)[None, :, None, None]
    angle = 2 * np.pi * ((a * np.arange(D // 2)) % D) / D
    return np.stack([np.cos(angle), np.sin(angle)], axis=1).astype(np.float32)


def xattn_ffn_kernel(nc, x, ctx, Wq, bq, Wk, bk, Wv, bv, Wo, bo, w_real, w_imag, bias, cos_sin, identity, out):
    B, S, D = x.shape
    KEYS = ctx.shape[1]
    HEADS = 16
    HD = D // HEADS
    C = D // P
    HALF = D // 2
    PAIRS = HEADS // 2
    HPC = P // HD
    TPB = S // P
    TILES = B * TPB
    TG = 2
    GROUPS = TPB // TG
    RING = 12
    VW = 2 * HD + 2
    SCALE = 1.0 / float(np.sqrt(np.float32(HD)))
    assert TPB == 8 and C == 4 and KEYS * 2 == P and B * KEYS == D and B > 2

    x_groups = x.rearrange("b (g p t) f -> (b g) p t f", p=P, t=TG)
    out_groups = out.rearrange("b (g p t) f -> (b g) p t f", p=P, t=TG)

    stack = ExitStack()
    with stack:
        def sb(name, shape, dt, where=stack):
            return where.enter_context(nc.sbuf_tensor(name, shape, dt))

        def ps(name, shape):
            return stack.enter_context(nc.psum_tensor(name, shape, F32))

        def sem(name):
            return stack.enter_context(nc.semaphore(name))

        key_stack = sb("key_stack", [P, HEADS, B, KEYS], F16)
        value_blocks = sb("value_blocks", [P, 2, B, PAIRS, VW], F16)
        WqT = sb("WqT", [P, 2, C, C, P], F16)
        WoT = sb("WoT", [P, 2, C, C, P], F16)
        ffn = sb("ffn", [P, 2, C, D], F16)
        bq_rows = sb("bq_rows", [P, D], F32)
        bo_rows = sb("bo_rows", [P, D], F32)
        bias_rows = sb("bias_rows", [P, D], F32)
        ident = sb("ident", [P, P], F32)
        bk_cols = sb("bk_cols", [P, C], F32)
        peaks = sb("peaks", [P, 3, 8], F32)
        powers = sb("powers", [P, 8], F32)
        gains = sb("gains", [P, 3, 8], F32)
        factors = sb("factors", [P, 4], F32)
        minus_half = sb("minus_half", [P, 1], F32)
        wide = sb("wide", [P, C, D], F32)

        most = sb("most", [P, 2, HEADS], F32)
        per_sum = sb("per_sum", [P, 2, HEADS], F32)
        stats = sb("stats", [P, 2, 2, 6], F32)
        moments = sb("moments", [P, 2, 4, 2], F32)
        vareps = sb("vareps", [P, 2, 4], F32)
        rstd = sb("rstd", [P, 2, 4], F32)
        minus_mean = sb("minus_mean", [P, 2, 4], F32)

        early = ExitStack()
        turned = sb("turned", [P, 2, 2, C, D], F32R, early)
        spectra = turned
        trig = sb("trig", [P, 3, 2, 2, 2, HALF], F32R, early)
        odd = sb("odd", [P, 2, HALF], F32, early)
        columns = sb("columns", [P, 2, 2, 2, 2, 2, P], F32R, early)
        sums = sb("sums", [P, 2, D], F32, early)
        bv_rows = sb("bv_rows", [P, D], F32, early)
        parts = sb("parts", [P, 2, C, D], F16, early)
        kv_parts = ffn
        keys = sb("keys", [P, C, D], F32, early)
        raw = sb("raw", [P, 3, C, D], F32, early)
        early.close()

        shifted = sb("shifted", [P, HEADS, KEYS], F32)
        prob = sb("prob", [P, HEADS * KEYS], F32)
        prob_parts = sb("prob_parts", [P, 2, 2, HEADS * KEYS], F16)
        probT = sb("probT", [P, 2, 2, PAIRS, P], F16)
        o_rows = sb("o_rows", [P, 2, D], F32)
        o_parts = sb("o_parts", [P, 2, 2, D], F16)
        oT = sb("oT", [P, 2, 2, C, P], F16)
        n2 = sb("n2", [P, 2, D], F32)
        n2_parts = sb("n2_parts", [P, 2, 2, D], F16)
        n2T = sb("n2T", [P, 2, 2, C, P], F16)
        q_sum = sb("q_sum", [P, 2, D], F32)
        q_parts = sb("q_parts", [P, 2, HEADS, 4, HD], F16)
        n1T = sb("n1T", [P, 2, 2, C, P], F16)
        n1_parts = sb("n1_parts", [P, 2, 2, D], F16)
        n1 = sb("n1", [P, 2, D], F32)
        qT = sb("qT", [P, 2, HEADS, P], F16)
        rows = sb("rows", [P, RING, TG, D], F32)

        ps_q = ps("ps_q", [P, D])
        ps_proj = ps("ps_proj", [P, D])
        ps_ffn = ps("ps_ffn", [P, D])
        ps_spare = ps("ps_spare", [P, D])
        ps_s = ps("ps_s", [P, 2, D])
        ps_o = ps("ps_o", [P, PAIRS, P])
        banks = [ps_q[:], ps_proj[:], ps_ffn[:], ps_spare[:], ps_s[:, 0, :], ps_s[:, 1, :],
                 ps_o[:, 0:4, :].rearrange("p a b -> p (a b)"), ps_o[:, 4:8, :].rearrange("p a b -> p (a b)")]

        ctx_in, wk_in, wv_in, trig_in, ident_in = map(sem, ("ctx_in", "wk_in", "wv_in", "trig_in", "ident_in"))
        real_in, imag_in, wq_in, wo_in = map(sem, ("real_in", "imag_in", "wq_in", "wo_in"))
        cols_in, bq_in, bv_in, rows_in = map(sem, ("cols_in", "bq_in", "bv_in", "rows_in"))
        turn_made, key_made, value_made, g_made, a_made = map(sem, ("turn_made", "key_made", "value_made", "g_made", "a_made"))
        turn_hi, turn_lo, key_kept, value_kept = map(sem, ("turn_hi", "turn_lo", "key_kept", "value_kept"))
        trig_hi, trig_lo, trig_neg, cols_hi, cols_lo = map(sem, ("trig_hi", "trig_lo", "trig_neg", "cols_hi", "cols_lo"))
        g_odd, g_sum, g_hi, g_lo, a_odd, a_sum = map(sem, ("g_odd", "g_sum", "g_hi", "g_lo", "a_odd", "a_sum"))
        peak_own, peak_all = ([sem(f"{name}_{col}") for col in range(7)] for name in ("peak_own", "peak_all"))
        chain = sem("chain")
        q_gain, k_gain, o_gain, v_gain, a_gain = map(sem, ("q_gain", "k_gain", "o_gain", "v_gain", "a_gain"))
        query_ready = sem("query_ready")
        part_hi, part_lo, kv_hi, kv_lo, weight_turned, keys_spread, values_spread = map(
            sem, ("part_hi", "part_lo", "kv_hi", "kv_lo", "weight_turned", "keys_spread", "values_spread"))
        filled, ones_set, ffn_hi, ffn_lo = map(sem, ("filled", "ones_set", "ffn_hi", "ffn_lo"))
        x_stats, x_moments, x_var_eps, x_rstd, x_shift, n1_made, n1_hi, n1_lo = map(
            sem, ("x_stats", "x_moments", "x_var_eps", "x_rstd", "x_shift", "n1_made", "n1_hi", "n1_lo"))
        q_made, q_kept, q_hi, q_lo, q_zero = map(sem, ("q_made", "q_kept", "q_hi", "q_lo", "q_zero"))
        s_made, s_max, s_shifted, p_made, p_hi, p_lo = map(
            sem, ("s_made", "s_max", "s_shifted", "p_made", "p_hi", "p_lo"))
        o_made, o_rec, o_kept, o_hi, o_lo = map(sem, ("o_made", "o_rec", "o_kept", "o_hi", "o_lo"))
        proj_made, xb_made, x2_made, x2_stats, x2_moments, x2_var_eps, x2_rstd, x2_shift = map(
            sem, ("proj_made", "xb_made", "x2_made", "x2_stats", "x2_moments", "x2_var_eps", "x2_rstd", "x2_shift"))
        n2_made, n2_hi, n2_lo, ffn_made, x2b_made, y_made = map(
            sem, ("n2_made", "n2_hi", "n2_lo", "ffn_made", "x2b_made", "y_made"))
        x_in, y_out = ([sem(f"{name}_{group}") for group in range(GROUPS)] for name in ("x_in", "y_out"))
        n1_turned, q_turned, p_turned, o_turned, n2_turned = (
            [sem(f"{name}_{turn}") for turn in range(2)]
            for name in ("n1_turned", "q_turned", "p_turned", "o_turned", "n2_turned"))

        def due(eng, *waits, alone=False):
            waits = [(semaphore, value) for semaphore, value in waits if not isinstance(value, int) or value > 0]
            assert all(isinstance(value, int) or value.min_val > 0 for _, value in waits)
            if alone and any(not isinstance(value, int) for _, value in waits):
                waits = [(semaphore, value if isinstance(value, int) else eng.to_reg(value)) for semaphore, value in waits]
                eng.wait_ge(waits[0][0], 1)
            for semaphore, value in waits:
                eng.wait_ge(semaphore, value)

        def steps(eng, step, first):
            for k in range(first, TPB):
                step(0, k)
            with eng.Fori(1, B - 1) as b:
                for k in range(TPB):
                    step(b, k)
            for k in range(TPB * (B - 1), TILES + STORE):
                step(0, k)

        def staged(*order):
            def step(b, k):
                for lag, stage in order:
                    if on(b, k - lag):
                        stage(b, k - lag)
            return step

        def on(b, k):
            return not isinstance(b, int) or 0 <= k < TILES

        def at(b, k):
            return b * TPB + k

        def slot_of(b, group):
            return (b * GROUPS + group + 4) % RING

        def row_tile(b, k):
            return rows[:, slot_of(b, k // TG), k % TG, :]

        PQ, PB, PK, PV, PO, PA, PBIAS = range(7)
        SCORES, PROJ, FFN, QUERY = range(4)

        block = stack.enter_context(nc.Block())

        def rounds(b, t, each=TPB):
            return b * (each // 2) + t // 2

        @block.sync
        def _(sp):
            for done in y_out:
                sp.sem_inc(done, 16)
            weight_rows = "(r p) f -> p r f"
            spectrum_rows = "(c p a) o -> a p c o"
            sp.dma_start(raw[:, 0], ctx.rearrange("b k f -> (b k) f").rearrange(weight_rows, p=P)).then_inc(ctx_in, 16)
            sp.dma_start(ident[:], identity).then_inc(ident_in, 16)
            sp.dma_start(raw[:, 1], Wk.rearrange(weight_rows, p=P)).then_inc(wk_in, 16)
            sp.dma_start(raw[:, 2], Wv.rearrange(weight_rows, p=P)).then_inc(wv_in, 16)
            sp.dma_start(wide[:].rearrange("p r n -> p (r n)"), cos_sin).then_inc(trig_in, 16)
            with nc.allow_non_contiguous_dma(reason="the keys' bias as columns, 2 KB"):
                sp.dma_start(bk_cols[:], bk.rearrange("(c p) -> p c", p=P)).then_inc(cols_in, 16)
            sp.dma_start(bq_rows[:], bq.partition_broadcast(P)).then_inc(bq_in, 16)
            sp.wait_ge(turn_made, C)
            for a in range(2):
                sp.dma_start(raw[:, 0, 2 * a:2 * a + 2, :], w_real.rearrange(spectrum_rows, p=P, a=2)[a]).then_inc(real_in, 16)
            sp.wait_ge(turn_made, 2 * C)
            for a in range(2):
                sp.dma_start(raw[:, 1, 2 * a:2 * a + 2, :], w_imag.rearrange(spectrum_rows, p=P, a=2)[a]).then_inc(imag_in, 16)
            sp.wait_ge(turn_made, 3 * C)
            sp.dma_start(raw[:, 2], Wq.rearrange(weight_rows, p=P)).then_inc(wq_in, 16)
            sp.dma_start(bv_rows[:], bv.partition_broadcast(P)).then_inc(bv_in, 16)
            sp.dma_start(bo_rows[:], bo.partition_broadcast(P)).then_inc(rows_in, 16)
            sp.dma_start(bias_rows[:], bias.partition_broadcast(P)).then_inc(rows_in, 16)

            def turn_weight(n, turned_weight):
                sp.wait_ge(part_lo, n + 1)
                if n == 0:
                    sp.dma_start(raw[:, 2], Wo.rearrange(weight_rows, p=P)).then_inc(wo_in, 16)
                sp.dma_start_transpose(turned_weight[:].rearrange("p a r c o -> p (a r c) o"),
                                       parts[:].rearrange("p a r f -> p (a r f)")).then_inc(weight_turned, 16)

            def stack_keys():
                sp.wait_ge(filled, 3)
                sp.wait_ge(kv_lo, 1)
                for h in range(HPC):
                    for row, part in enumerate((HIGH, HIGH, LOW)):
                        sp.dma_start(key_stack[HD * row:HD * row + HD, h::HPC].rearrange("p c b n -> p c (b n)"),
                                     kv_parts[HD * h:HD * h + HD, part]).then_inc(keys_spread, 16)

            def turn_q(b, t):
                if t == 0 and isinstance(b, int):
                    sp.wait_ge(q_zero, 1)
                due(sp, (q_lo, at(b, t) + 1),
                    (s_made, at(b, t) - 1), alone=True)
                sp.dma_start_transpose(qT[:, t % 2], q_parts[:, t % 2].rearrange("p h a d -> p (h a d)")).then_inc(q_turned[t % 2], 16)

            def turn_n2(b, t):
                due(sp, (n2_lo, at(b, t) + 1),
                    (ffn_made, at(b, t) - 1), alone=True)
                sp.dma_start_transpose(n2T[:, t % 2].rearrange("p a c n -> p (a c) n"),
                                       n2_parts[:, t % 2].rearrange("p a f -> p (a f)")).then_inc(n2_turned[t % 2], 16)

            def store(b, t):
                if t % TG == TG - 1:
                    group = t // TG
                    due(sp, (y_made, at(b, t) + 1), alone=True)
                    sp.dma_start(out_groups[b * GROUPS + group], rows[:, slot_of(b, group)]).then_inc(y_out[group % GROUPS], 16)

            def load(b, t):
                if t % TG == 0:
                    group = t // TG
                    if t == 0 and isinstance(b, int):
                        sp.wait_ge(cols_lo, 8)
                    if t == TPB and isinstance(b, int):
                        sp.wait_ge(weight_turned, 32)
                        sp.wait_ge(kv_lo, 1)
                    before = group - RING
                    due(sp, (y_out[before % GROUPS], (b + before // GROUPS + 2) * 16), alone=True)
                    sp.dma_start(rows[:, slot_of(b, group)], x_groups[b * GROUPS + group]).then_inc(x_in[group % GROUPS], 16)

            def turn_n1(b, t):
                if t == 0 and isinstance(b, int):
                    sp.wait_ge(g_made, 2 * C)
                due(sp, (n1_lo, at(b, t) + 1),
                    (q_made, at(b, t) - 1), alone=True)
                sp.dma_start_transpose(n1T[:, t % 2].rearrange("p a c n -> p (a c) n"),
                                       n1_parts[:, t % 2].rearrange("p a f -> p (a f)")).then_inc(n1_turned[t % 2], 16)

            def turn_o(b, t):
                due(sp, (o_lo, at(b, t) + 1),
                    (proj_made, at(b, t) - 1), alone=True)
                sp.dma_start_transpose(oT[:, t % 2].rearrange("p a c n -> p (a c) n"),
                                       o_parts[:, t % 2].rearrange("p a f -> p (a f)")).then_inc(o_turned[t % 2], 16)

            def turn_p(b, t):
                due(sp, (p_lo, at(b, t) + 1),
                    (o_made, at(b, t) - 1), alone=True)
                sp.dma_start_transpose(probT[:, t % 2].rearrange("p a g n -> p (a g) n"),
                                       prob_parts[:, t % 2].rearrange("p a f -> p (a f)")).then_inc(p_turned[t % 2], 16)

            step = staged((-8, load), (8, store), (4, turn_o), (-4, turn_n1), (-1, turn_q), (6, turn_n2),
                          (1, turn_p))
            turn_weight(0, WqT)
            stack_keys()
            for k in range(-8, -1):
                step(0, k)
            turn_weight(1, WoT)
            for k in range(-1, 4):
                step(0, k)
            steps(sp, step, 4)
            for done in y_out:
                sp.wait_ge(done, (B + 1) * 16)

        @block.gpsimd
        def _(pool):
            pool.memset(minus_half[:], -0.5).then_inc(filled, 1)
            pool.memset(value_blocks[:].rearrange("p a b g w -> p (a b g w)").bitcast(F32), 0.0).then_inc(filled, 1)
            pool.memset(key_stack[:].rearrange("p h b n -> p (h b n)").bitcast(F32), 0.0).then_inc(filled, 1)
            pool.wait_ge(filled, 3)
            for head in range(2):
                rows_of = slice(head * KEYS, head * KEYS + KEYS)
                pool.memset(value_blocks[rows_of, HIGH, :, :, 2 * HD + head:2 * HD + head + 1], 1.0).then_inc(ones_set, 1)
            pool.wait_ge(ones_set, 2)

            def peak_of_all(col):
                pool.wait_ge(peak_own[col], 1)
                pool.partition_all_reduce(peaks[:, 1, col:col + 1], peaks[:, 0, col:col + 1], P, RMAX).then_inc(peak_all[col], 1)

            def rest(to, whole, high):
                return pool.tensor_tensor(to, whole, high, ALU.subtract)

            def columns_rest(n):
                for which in range(2):
                    pool.wait_ge(cols_hi, 2 * n + which + 1)
                    rest(columns[:, n % 2, which, LOW].rearrange("p a c o -> p (a c) o"),
                         raw[:, which].rearrange("p r (o a) -> p r o a", a=2)[:, :, P * (n % 2):P * (n % 2) + P, n // 2],
                         columns[:, n % 2, which, HIGH].rearrange("p a c o -> p (a c) o").bitcast(F32)).then_inc(cols_lo, 1)

            def spectrum_rest(n):
                pool.wait_ge(g_hi, n + 1)
                rest(spectra[:, n % 2, LOW, n // 2], sums[:, n % 2],
                     spectra[:, n % 2, HIGH, n // 2].bitcast(F32)).then_inc(g_lo, 1)

            def deviation(b, t, moments_made, sum_made, done, norm):
                slot = slice(t % 4, t % 4 + 1)
                due(pool, (moments_made, at(b, t) + 1), alone=True)
                pool.tensor_scalar(vareps[:, norm, slot], moments[:, norm, t % 4, 1:2], EPS, 2.0 ** (-2 * LN_GAIN),
                                   ALU.add, ALU.mult).then_inc(sum_made, 1)
                due(pool, (sum_made, at(b, t) + 1), alone=True)
                pool.tensor_tensor(rstd[:, norm, slot], vareps[:, norm, slot], minus_half[:], ALU.pow).then_inc(done, 1)

            def n2_rest(b, t):
                due(pool, (n2_hi, at(b, t) + 1), alone=True)
                rest(n2_parts[:, t % 2, LOW], n2[:, t % 2], n2_parts[:, t % 2, HIGH]).then_inc(n2_lo, 1)

            def shift_of(b, t, deviation_made, done, norm):
                slot = slice(t % 4, t % 4 + 1)
                due(pool, (deviation_made, at(b, t) + 1), alone=True)
                pool.tensor_scalar(minus_mean[:, norm, slot], moments[:, norm, t % 4, 0:1], rstd[:, norm, slot], -1.0,
                                   ALU.mult, ALU.mult).then_inc(done, 1)

            def deviation1(b, t):
                deviation(b, t, x_moments, x_var_eps, x_rstd, 0)
                shift_of(b, t, x_rstd, x_shift, 0)

            def deviation2(b, t):
                deviation(b, t, x2_moments, x2_var_eps, x2_rstd, 1)
                shift_of(b, t, x2_rstd, x2_shift, 1)

            def zero_q():
                pool.wait_ge(a_made, C)
                pool.wait_ge(a_sum, 2 * C)
                pool.memset(q_parts[:, :, :, 3, :], 0.0).then_inc(q_zero, 1)

            def add_bias(b, t):
                due(pool, (n2_made, at(b, t) + 1), alone=True)
                row = row_tile(b, t)
                pool.tensor_tensor(row, row, bias_rows[:], ALU.add).then_inc(x2b_made, 1)

            def n1_rest(b, t):
                due(pool, (n1_hi, at(b, t) + 1), alone=True)
                rest(n1_parts[:, t % 2, LOW], n1[:, t % 2], n1_parts[:, t % 2, HIGH]).then_inc(n1_lo, 1)

            def add_bo(b, t):
                if t == 0 and isinstance(b, int):
                    pool.wait_ge(rows_in, 32)
                due(pool, (n1_made, at(b, t) + 1), alone=True)
                row = row_tile(b, t)
                pool.tensor_tensor(row, row, bo_rows[:], ALU.add).then_inc(xb_made, 1)

            def q_rest(b, t):
                due(pool, (q_hi, at(b, t) + 1), alone=True)
                rest(q_parts[:, t % 2, :, 1], q_sum[:, t % 2].rearrange("p (h d) -> p h d", d=HD),
                     q_parts[:, t % 2, :, 0]).then_inc(q_lo, 1)

            step = staged((7, n2_rest), (-4, n1_rest), (6, deviation2), (-2, add_bo), (-1, q_rest), (7, add_bias),
                          (-6, deviation1))
            peak_of_all(PBIAS)
            columns_rest(0)
            peak_of_all(PQ)
            columns_rest(1)
            peak_of_all(PK)
            columns_rest(2)
            peak_of_all(PO)
            spectrum_rest(0)
            spectrum_rest(1)
            peak_of_all(PV)
            spectrum_rest(2)
            columns_rest(3)
            for n in range(3, 7):
                spectrum_rest(n)
            step(0, -6)
            spectrum_rest(7)
            for k in range(-5, 0):
                step(0, k)
            zero_q()
            peak_of_all(PA)
            for k in range(4):
                step(0, k)
            steps(pool, step, 4)

        @block.scalar
        def _(act):
            def high(to, whole, col=None):
                if col is None:
                    return act.activation(to, whole, ACT.Copy)
                return act.activation(to, whole, ACT.Identity, bias=0.0, scale=gains[:, 1, col:col + 1])

            def turn(n):
                if n >= 2 * C:
                    act.wait_ge(key_made, C)
                act.wait_ge(turn_made, n + 1)
                high(turned[:, min(n // C, 1), HIGH, n % C], banks[n % 8 if n < 8 else 4 + n % C]).then_inc(turn_hi, 1)

            def column_parts(n):
                if n == 0:
                    act.wait_ge(real_in, 32)
                    act.wait_ge(imag_in, 32)
                if n >= 2:
                    act.wait_ge(g_made, 2 * n - 2)
                for which in range(2):
                    high(columns[:, n % 2, which, HIGH].rearrange("p a c o -> p (a c) o"),
                         raw[:, which].rearrange("p r (o a) -> p r o a", a=2)[:, :, P * (n % 2):P * (n % 2) + P, n // 2]
                         ).then_inc(cols_hi, 1)

            def spectrum_odd(n):
                act.wait_ge(g_made, n + 1)
                if n >= 2:
                    act.wait_ge(g_sum, 2 * n - 2)
                act.activation(odd[:, n % 2], banks[n][:, HALF:], ACT.Copy).then_inc(g_odd, 1)

            def spectrum_high(n):
                act.wait_ge(g_sum, 2 * n + 2)
                if n == 0:
                    act.wait_ge(value_made, C)
                high(spectra[:, n % 2, HIGH, n // 2], sums[:, n % 2]).then_inc(g_hi, 1)

            def split(to, whole, col, ready, done):
                act.wait_ge(ready, 1)
                high(to[:, HIGH], whole, col).then_inc(done, 1)

            def take_key(j):
                if j == 0:
                    act.wait_ge(cols_in, 16)
                act.wait_ge(key_made, j + 1)
                act.activation(keys[:, j], banks[j], ACT.Identity, bias=bk_cols[:, j:j + 1]).then_inc(key_kept, 1)

            def minus_cos(part, ready):
                act.wait_ge(ready, 1)
                act.mul(trig_flat[:, 2, part], trig_flat[:, 0, part].bitcast(F32), -1.0).then_inc(trig_neg, 1)

            tables_in = wide[:].rearrange("p (t r) n -> p t (r n)", t=2)
            trig_flat = trig[:].rearrange("p t s a c n -> p t s (a c n)")

            def tables_high():
                act.wait_ge(trig_in, 16)
                high(trig_flat[:, 0:2, HIGH], tables_in).then_inc(trig_hi, 1)

            def split_wo():
                act.wait_ge(weight_turned, 16)
                split(parts, raw[:, 2], PO, o_gain, part_hi)

            def split_values():
                act.wait_ge(keys_spread, 3 * HPC * 16)
                split(kv_parts, wide[:], PV, v_gain, kv_hi)

            def matrix(n):
                act.wait_ge(a_made, n + 1)
                if n >= 2:
                    act.wait_ge(a_sum, 2 * n - 2)
                act.activation(odd[:, n % 2], banks[n][:, HALF:], ACT.Copy).then_inc(a_odd, 1)

            def first_norm(b, t):
                if t == 0 and isinstance(b, int):
                    act.wait_ge(g_made, 2 * C)
                due(act, (x_shift, at(b, t) + 1))
                due(act, (n1_lo, at(b, t) - 1))
                act.activation(n1[:, t % 2], row_tile(b, t), ACT.Identity, bias=minus_mean[:, 0, t % 4:t % 4 + 1],
                               scale=rstd[:, 0, t % 4:t % 4 + 1]).then_inc(n1_made, 1)

            def second_norm(b, t):
                due(act, (x2_shift, at(b, t) + 1))
                due(act, (n2_lo, at(b, t) - 1))
                act.activation(n2[:, t % 2], row_tile(b, t), ACT.Identity, bias=minus_mean[:, 1, t % 4:t % 4 + 1],
                               scale=rstd[:, 1, t % 4:t % 4 + 1]).then_inc(n2_made, 1)

            def n2_high(b, t):
                due(act, (n2_made, at(b, t) + 1))
                due(act, (n2_turned[t % 2], rounds(b, t) * 16))
                high(n2_parts[:, t % 2, HIGH], n2[:, t % 2]).then_inc(n2_hi, 1)

            def n1_high(b, t):
                if t == 0 and isinstance(b, int):
                    act.wait_ge(g_made, 2 * C)
                due(act, (n1_made, at(b, t) + 1))
                due(act, (n1_turned[t % 2], rounds(b, t) * 16))
                high(n1_parts[:, t % 2, HIGH], n1[:, t % 2]).then_inc(n1_hi, 1)

            def exponentials(b, t):
                if t == 0 and isinstance(b, int):
                    act.wait_ge(query_ready, 3)
                due(act, (s_shifted, at(b, t) + 1))
                due(act, (p_lo, at(b, t)))
                act.activation(prob[:], shifted[:].rearrange("p h n -> p (h n)"), ACT.Exp,
                               scale=factors[:, SCORES:SCORES + 1]).then_inc(p_made, 1)

            def p_high(b, t):
                due(act, (p_made, at(b, t) + 1))
                due(act, (p_turned[t % 2], rounds(b, t) * 16))
                act.activation(prob_parts[:, t % 2, HIGH], prob[:], ACT.Copy, scale=2.0 ** P_GAIN).then_inc(p_hi, 1)

            def q_high(b, t):
                due(act, (q_kept, at(b, t) + 1))
                due(act, (q_turned[t % 2], rounds(b, t) * 16))
                high(q_parts[:, t % 2, :, 0:3:2], q_sum[:, t % 2].rearrange("p (h d) -> p h d", d=HD)
                     .unsqueeze(2).to_broadcast([P, HEADS, 2, HD])).then_inc(q_hi, 1)

            def o_high(b, t):
                due(act, (o_kept, at(b, t) + 1))
                due(act, (o_turned[t % 2], rounds(b, t) * 16))
                high(o_parts[:, t % 2, HIGH], o_rows[:, t % 2]).then_inc(o_hi, 1)

            step = staged((-5, first_norm), (1, exponentials), (1, p_high), (-5, n1_high), (6, second_norm),
                          (6, n2_high), (3, o_high), (-2, q_high))

            def matrix_high():
                act.wait_ge(values_spread, 8)
                split(ffn, wide[:], PA, a_gain, ffn_hi)

            for n in range(8):
                turn(n)
            tables_high()
            take_key(0)
            minus_cos(HIGH, trig_hi)
            take_key(1)
            minus_cos(LOW, trig_lo)
            column_parts(0)
            take_key(2)
            take_key(3)
            for n in range(8, 11):
                turn(n)
            spectrum_odd(0)
            turn(11)
            split(parts, raw[:, 2], PQ, q_gain, part_hi)
            spectrum_odd(1)
            column_parts(1)
            split(kv_parts, keys[:], PK, k_gain, kv_hi)
            spectrum_high(0)
            column_parts(2)
            spectrum_high(1)
            spectrum_odd(2)
            split_wo()
            column_parts(3)
            spectrum_odd(3)
            spectrum_high(2)
            spectrum_high(3)
            spectrum_odd(4)
            spectrum_high(4)
            split_values()
            spectrum_odd(5)
            spectrum_odd(6)
            spectrum_high(5)
            spectrum_high(6)
            spectrum_odd(7)
            spectrum_high(7)
            for k in range(-5, -2):
                step(0, k)
            for n in range(4):
                matrix(n)
            for k in range(-2, 2):
                step(0, k)
            matrix_high()
            step(0, 2)
            step(0, 3)
            steps(act, step, 4)

        @block.vector
        def _(dve):
            links = [0]

            def link(instruction):
                links[0] += 1
                instruction.then_inc(chain, 1)
                dve.wait_ge(chain, links[0])

            def rest(to, whole, high):
                return dve.tensor_tensor(to, whole, high, ALU.subtract)

            def turn(n):
                dve.wait_ge(turn_hi, n + 1)
                rest(turned[:, min(n // C, 1), LOW, n % C], banks[n % 8 if n < 8 else 4 + n % C],
                     turned[:, min(n // C, 1), HIGH, n % C].bitcast(F32)).then_inc(turn_lo, 1)

            def own_peak(col, whole):
                dve.tensor_reduce(peaks[:, 0, col:col + 1], whole, AX.X, ALU.max,
                                  apply_absolute_value=True).then_inc(peak_own[col], 1)

            def power(col, clipped=False):
                if not clipped:
                    dve.wait_ge(peak_all[col], 1)
                    link(dve.tensor_scalar(peaks[:, 2, col:col + 1], peaks[:, 1, col:col + 1], 1e-30, None, ALU.max))
                link(dve.tensor_scalar(powers[:, col:col + 1].bitcast(I32), peaks[:, 2, col:col + 1].bitcast(I32),
                                       EXPONENT_BITS, None, ALU.bitwise_and))
                link(dve.reciprocal(gains[:, 0, col:col + 1], powers[:, col:col + 1]))

            def gain(col, ready):
                dve.tensor_scalar(gains[:, 1, col:col + 1], gains[:, 0, col:col + 1], 2.0 ** TOP, None,
                                  ALU.mult).then_inc(ready, 1)

            def split_rest(n, to, whole, high, col, hi_done, lo_done):
                dve.wait_ge(hi_done, n + 1)
                dve.scalar_tensor_tensor(out=to, in0=whole, scalar=gains[:, 1, col:col + 1], in1=high,
                                         op0=ALU.mult, op1=ALU.subtract).then_inc(lo_done, 1)

            def spread_values():
                dve.wait_ge(ones_set, 2)
                dve.wait_ge(kv_lo, 2)
                for part in range(2):
                    for b in range(2):
                        for h in range(2):
                            dve.tensor_copy(
                                value_blocks[KEYS * h:KEYS * h + KEYS, part, b::2, :, HD * h:HD * h + HD],
                                kv_parts[KEYS * b:KEYS * b + KEYS, part].rearrange("p r (g h d) -> p r g h d", h=2, d=HD)[:, :, :, h]
                            ).then_inc(values_spread, 1)

            def take_value(r):
                if r == 0:
                    dve.wait_ge(bv_in, 16)
                    dve.wait_ge(trig_lo, 1)
                dve.wait_ge(value_made, r + 1)
                dve.tensor_tensor(wide[:, r], banks[4 + r], bv_rows[:], ALU.add).then_inc(value_kept, 1)

            def spectrum(n):
                dve.wait_ge(g_odd, n + 1)
                if n >= 2:
                    dve.wait_ge(g_lo, n - 1)
                for half, op in enumerate((ALU.add, ALU.subtract)):
                    dve.tensor_tensor(sums[:, n % 2, HALF * half:HALF * half + HALF], banks[n][:, :HALF], odd[:, n % 2],
                                      op).then_inc(g_sum, 1)

            def tables_rest():
                dve.wait_ge(trig_hi, 1)
                tables_in = wide[:].rearrange("p (t r) n -> p t (r n)", t=2)
                trig_flat = trig[:].rearrange("p t s a c n -> p t s (a c n)")
                rest(trig_flat[:, 0:2, LOW], tables_in, trig_flat[:, 0:2, HIGH].bitcast(F32)).then_inc(trig_lo, 1)

            def bias_peak():
                dve.wait_ge(bq_in, 16)
                own_peak(PBIAS, bq_rows[:])

            def weight_peak(col, arrived):
                dve.wait_ge(arrived, 16)
                own_peak(col, raw[:, 2].rearrange("p c n -> p (c n)"))

            def keys_peak():
                dve.wait_ge(key_kept, C)
                own_peak(PK, keys[:].rearrange("p c n -> p (c n)"))

            def values_peak():
                dve.wait_ge(value_kept, C)
                own_peak(PV, wide[:].rearrange("p c n -> p (c n)"))

            def query_factors():
                power(PBIAS)
                power(PQ)
                gain(PQ, q_gain)
                link(dve.scalar_tensor_tensor(out=peaks[:, 2, PB:PB + 1], in0=peaks[:, 2, PQ:PQ + 1], scalar=float(D),
                                              in1=peaks[:, 2, PBIAS:PBIAS + 1], op0=ALU.mult, op1=ALU.add))
                power(PB, clipped=True)
                link(dve.tensor_scalar(gains[:, 1, PB:PB + 1], gains[:, 0, PB:PB + 1], 2.0 ** (TOP + 1), None, ALU.mult))
                dve.tensor_scalar(bq_rows[:], bq_rows[:], gains[:, 1, PB:PB + 1], None, ALU.mult).then_inc(query_ready, 1)
                dve.tensor_scalar(factors[:, QUERY:QUERY + 1], powers[:, PQ:PQ + 1], gains[:, 1, PB:PB + 1],
                                  2.0 ** -(TOP + LN_GAIN), ALU.mult, ALU.mult).then_inc(query_ready, 1)

            def score_factor():
                power(PK)
                gain(PK, k_gain)
                dve.tensor_scalar(factors[:, SCORES:SCORES + 1], powers[:, PB:PB + 1], powers[:, PK:PK + 1],
                                  SCALE * 2.0 ** -(2 * TOP + 1), ALU.mult, ALU.mult).then_inc(query_ready, 1)

            def projection_gain():
                power(PO)
                gain(PO, o_gain)

            def projection_factor():
                power(PV)
                gain(PV, v_gain)
                link(dve.tensor_scalar(factors[:, PROJ:PROJ + 1], powers[:, PV:PV + 1], powers[:, PO:PO + 1],
                                       2.0 ** -(2 * TOP), ALU.mult, ALU.mult))

            def result(b, t):
                row = row_tile(b, t)
                due(dve, (ffn_made, at(b, t) + 1))
                due(dve, (x2b_made, at(b, t) + 1))
                dve.scalar_tensor_tensor(out=row, in0=ps_ffn[:], scalar=factors[:, FFN:FFN + 1], in1=row,
                                         op0=ALU.mult, op1=ALU.add).then_inc(y_made, 1)

            def take_q(b, t):
                if t == 0 and isinstance(b, int):
                    dve.wait_ge(query_ready, 3)
                    dve.wait_ge(a_sum, 2 * C)
                due(dve, (q_made, at(b, t) + 1))
                due(dve, (q_lo, at(b, t) - 1))
                dve.scalar_tensor_tensor(out=q_sum[:, t % 2], in0=ps_q[:], scalar=factors[:, QUERY:QUERY + 1], in1=bq_rows[:],
                                         op0=ALU.mult, op1=ALU.add).then_inc(q_kept, 1)

            def maximum(b, t):
                due(dve, (s_made, at(b, t) + 1))
                scores = ps_s[:].rearrange("p a (h n) -> p (a h) n", n=KEYS)
                dve.tensor_reduce(most[:, t % 2], scores, AX.X, ALU.max).then_inc(s_max, 1)

            def shift(b, t):
                scores = ps_s[:].rearrange("p a (h n) -> p (a h) n", n=KEYS)
                due(dve, (s_max, at(b, t) + 1))
                due(dve, (p_made, at(b, t)))
                dve.tensor_tensor(shifted[:], scores, most[:, t % 2].unsqueeze(2).to_broadcast([P, HEADS, KEYS]),
                                  ALU.subtract).then_inc(s_shifted, 1)

            def stat1(b, t):
                if t % TG == 0:
                    due(dve, (x_in[t // TG % GROUPS], (b + t // TG // GROUPS + 1) * 16), alone=True)
                dve.bn_stats(stats[:, 0, t % 2], row_tile(b, t)).then_inc(x_stats, 1)

            def moments1(b, t):
                due(dve, (x_stats, at(b, t) + 1), alone=True)
                dve.bn_aggr(moments[:, 0, t % 4], stats[:, 0, t % 2]).then_inc(x_moments, 1)

            def reciprocals(b, t):
                due(dve, (o_made, at(b, t) + 1))
                dve.reciprocal(per_sum[:, t % 2].rearrange("p (g h) -> p g h", h=2),
                               ps_o[:, :, 2 * HD:VW]).then_inc(o_rec, 1)

            def take_o(b, t):
                due(dve, (o_rec, at(b, t) + 1))
                due(dve, (o_lo, at(b, t) - 1))
                dve.tensor_tensor(
                    o_rows[:, t % 2].rearrange("p (g h d) -> p g h d", h=2, d=HD),
                    ps_o[:, :, 0:2 * HD].rearrange("p g (h d) -> p g h d", h=2),
                    per_sum[:, t % 2].rearrange("p (g h) -> p g h", h=2).unsqueeze(3).to_broadcast([P, PAIRS, 2, HD]),
                    ALU.mult).then_inc(o_kept, 1)

            def p_rest(b, t):
                due(dve, (p_hi, at(b, t) + 1))
                dve.scalar_tensor_tensor(out=prob_parts[:, t % 2, LOW], in0=prob[:], scalar=2.0 ** P_GAIN,
                                         in1=prob_parts[:, t % 2, HIGH], op0=ALU.mult,
                                         op1=ALU.subtract).then_inc(p_lo, 1)

            def o_rest(b, t):
                due(dve, (o_hi, at(b, t) + 1))
                rest(o_parts[:, t % 2, LOW], o_rows[:, t % 2], o_parts[:, t % 2, HIGH]).then_inc(o_lo, 1)

            def residual(b, t):
                row = row_tile(b, t)
                due(dve, (proj_made, at(b, t) + 1))
                due(dve, (xb_made, at(b, t) + 1))
                dve.scalar_tensor_tensor(out=row, in0=ps_proj[:], scalar=factors[:, PROJ:PROJ + 1], in1=row,
                                         op0=ALU.mult, op1=ALU.add).then_inc(x2_made, 1)

            def stat2(b, t):
                due(dve, (x2_made, at(b, t) + 1), alone=True)
                dve.bn_stats(stats[:, 1, t % 2], row_tile(b, t)).then_inc(x2_stats, 1)

            def moments2(b, t):
                due(dve, (x2_stats, at(b, t) + 1), alone=True)
                dve.bn_aggr(moments[:, 1, t % 4], stats[:, 1, t % 2]).then_inc(x2_moments, 1)

            step = staged((-6, stat1), (8, result), (1, maximum), (1, shift), (3, reciprocals), (-2, take_q),
                          (3, take_o), (4, o_rest), (5, residual), (-6, moments1), (1, p_rest), (5, stat2),
                          (5, moments2))

            def matrix(n):
                dve.wait_ge(a_odd, n + 1)
                for half, op in enumerate((ALU.add, ALU.subtract)):
                    dve.tensor_tensor(wide[:, n, HALF * half:HALF * half + HALF], banks[n][:, :HALF], odd[:, n % 2],
                                      op).then_inc(a_sum, 1)

            def matrix_peak():
                dve.wait_ge(a_sum, 2 * C)
                own_peak(PA, wide[:].rearrange("p c n -> p (c n)"))

            def matrix_gain():
                power(PA)
                gain(PA, a_gain)
                link(dve.tensor_scalar(factors[:, FFN:FFN + 1], powers[:, PA:PA + 1], 2.0 ** -(TOP + LN_GAIN) / D, None,
                                       ALU.mult))

            def matrix_rest():
                split_rest(0, ffn[:, LOW], wide[:], ffn[:, HIGH], PA, ffn_hi, ffn_lo)

            for n in range(8):
                turn(n)
            tables_rest()
            bias_peak()
            weight_peak(PQ, wq_in)
            for n in range(8, 12):
                turn(n)
            query_factors()
            keys_peak()
            split_rest(0, parts[:, LOW], raw[:, 2], parts[:, HIGH], PQ, part_hi, part_lo)
            spectrum(0)
            score_factor()
            spectrum(1)
            split_rest(0, kv_parts[:, LOW], keys[:], kv_parts[:, HIGH], PK, kv_hi, kv_lo)
            take_value(0)
            weight_peak(PO, wo_in)
            for n in range(1, 4):
                take_value(n)
            projection_gain()
            values_peak()
            spectrum(2)
            spectrum(3)
            split_rest(1, parts[:, LOW], raw[:, 2], parts[:, HIGH], PO, part_hi, part_lo)
            spectrum(4)
            projection_factor()
            split_rest(1, kv_parts[:, LOW], wide[:], kv_parts[:, HIGH], PV, kv_hi, kv_lo)
            spectrum(5)
            spectrum(6)
            spread_values()
            step(0, -6)
            spectrum(7)
            for k in range(-5, -2):
                step(0, k)
            for n in range(4):
                matrix(n)
            step(0, -2)
            matrix_peak()
            step(0, -1)
            step(0, 0)
            matrix_gain()
            step(0, 1)
            step(0, 2)
            matrix_rest()
            step(0, 3)
            steps(dve, step, 4)

        @block.tensor
        def _(pe):
            def turn(n, slot):
                for r in range(C):
                    last = pe.transpose(banks[n if n < 2 * C else n - C][:, P * r:P * r + P],
                                        raw[:, slot, r, P * (n % C):P * (n % C) + P], ident[:])
                last.then_inc(turn_made, 1)

            pe.wait_ge(ident_in, 16)
            for slot, arrived in enumerate((ctx_in, wk_in, wv_in)):
                pe.wait_ge(arrived, 16)
                for n in range(C * slot, C * slot + C):
                    if slot == 2:
                        pe.wait_ge(turn_lo, n - C + 1)
                    turn(n, slot)
            def key_products():
                for j in range(C):
                    for c in range(C):
                        for i, (left, right) in enumerate(PASSES):
                            last = pe.matmul(banks[j], turned[:, 1, left, c, P * j:P * j + P], turned[:, 0, right, c],
                                             start=(c == 0 and i == 0), stop=(c == C - 1 and i == 2))
                    last.then_inc(key_made, 1)

            def value_products(r):
                pe.wait_ge(turn_lo, 3 * C)
                for c in range(C):
                    for i, (left, right) in enumerate(PASSES):
                        last = pe.matmul(banks[4 + r], turned[:, 0, left, c, P * r:P * r + P], turned[:, 1, right, c],
                                         start=(c == 0 and i == 0), stop=(c == C - 1 and i == 2))
                last.then_inc(value_made, 1)

            def spectrum(n):
                quarter, imaginary = n // 2, n % 2
                if n == 0:
                    pe.wait_ge(trig_neg, 2)
                if n in (0, 2):
                    pe.wait_ge(key_kept, n + 2)
                if n >= 4:
                    pe.wait_ge(value_kept, n - 3)
                if not imaginary:
                    pe.wait_ge(cols_lo, 2 * quarter + 2)
                for parity in range(2):
                    products = [(which, table, c, left, right)
                                for which, table in enumerate((1, 2) if imaginary else (0, 1))
                                for c in range(2) for left, right in PASSES]
                    for i, (which, table, c, left, right) in enumerate(products):
                        last = pe.matmul(banks[n][:, HALF * parity:HALF * parity + HALF],
                                         columns[:, quarter % 2, which, left, parity, c],
                                         trig[:, table, right, parity, c],
                                         start=(i == 0), stop=(i == len(products) - 1))
                last.then_inc(g_made, 1)

            def matrix(parity):
                pe.wait_ge(g_lo, C * parity + C)
                for n in range(C):
                    products = [(which, c, left, right) for c in range(2) for which in range(2) for left, right in PASSES]
                    for i, (which, c, left, right) in enumerate(products):
                        last = pe.matmul(banks[n][:, HALF * parity:HALF * parity + HALF],
                                         spectra[:, which, left, 2 * parity + c, P * n:P * n + P],
                                         trig[:, which, right, parity, c],
                                         start=(i == 0), stop=(i == len(products) - 1))
                    if parity == 1:
                        last.then_inc(a_made, 1)

            def scores(b, t):
                if t == 0 and isinstance(b, int):
                    pe.wait_ge(keys_spread, 3 * HPC * 16)
                due(pe, (q_turned[t % 2], rounds(b, t) * 16 + 16))
                due(pe, (s_shifted, at(b, t)))
                for h in range(HEADS):
                    last = pe.matmul(ps_s[:, h // 8, KEYS * (h % 8):KEYS * (h % 8) + KEYS], qT[:, t % 2, h],
                                     key_stack[:, h, b + t // TPB], start=True, stop=True)
                last.then_inc(s_made, 1)

            def queries(b, t):
                if t == 0 and isinstance(b, int):
                    pe.wait_ge(weight_turned, 16)
                    pe.wait_ge(a_sum, 2)
                due(pe, (n1_turned[t % 2], rounds(b, t) * 16 + 16))
                due(pe, (q_kept, at(b, t)))
                for c in range(C):
                    for i, (left, right) in enumerate(PASSES):
                        last = pe.matmul(ps_q[:], n1T[:, t % 2, left, c], WqT[:, right, :, c, :],
                                         start=(c == 0 and i == 0), stop=(c == C - 1 and i == 2))
                last.then_inc(q_made, 1)

            def values(b, t):
                if t == 0 and isinstance(b, int):
                    pe.wait_ge(values_spread, 8)
                due(pe, (p_turned[t % 2], rounds(b, t) * 16 + 16))
                due(pe, (o_kept, at(b, t)))
                for g in range(PAIRS):
                    for i, (left, right) in enumerate(PASSES):
                        width = VW if right == HIGH else 2 * HD
                        last = pe.matmul(ps_o[:, g, :width], probT[:, t % 2, left, g],
                                         value_blocks[:, right, b + t // TPB, g, :width], start=(i == 0), stop=(i == 2))
                last.then_inc(o_made, 1)

            def project(b, t):
                if t == 0 and isinstance(b, int):
                    pe.wait_ge(weight_turned, 32)
                    pe.wait_ge(a_sum, 2 * C)
                due(pe, (o_turned[t % 2], rounds(b, t) * 16 + 16))
                due(pe, (x2_made, at(b, t)))
                for c in range(C):
                    for i, (left, right) in enumerate(PASSES):
                        last = pe.matmul(ps_proj[:], oT[:, t % 2, left, c], WoT[:, right, :, c, :],
                                         start=(c == 0 and i == 0), stop=(c == C - 1 and i == 2))
                last.then_inc(proj_made, 1)

            def forward(b, t):
                if t == 0 and isinstance(b, int):
                    pe.wait_ge(ffn_lo, 1)
                due(pe, (n2_turned[t % 2], rounds(b, t) * 16 + 16))
                due(pe, (y_made, at(b, t)))
                for c in range(C):
                    for i, (left, right) in enumerate(PASSES):
                        last = pe.matmul(ps_ffn[:], n2T[:, t % 2, left, c], ffn[:, right, c],
                                         start=(c == 0 and i == 0), stop=(c == C - 1 and i == 2))
                last.then_inc(ffn_made, 1)

            step = staged((1, scores), (-2, queries), (3, values), (5, project), (7, forward))
            key_products()
            spectrum(0)
            spectrum(1)
            for n in range(4):
                value_products(n)
            for n in range(2, 8):
                spectrum(n)
            matrix(0)
            matrix(1)
            for k in range(-2, 4):
                step(0, k)
            steps(pe, step, 4)


_INS = ["x", "ctx_1024", "L0_xattn_Wq", "L0_xattn_bq", "L0_xattn_Wk", "L0_xattn_bk", "L0_xattn_Wv", "L0_xattn_bv",
        "L0_xattn_Wo", "L0_xattn_bo", "L0_ffn_w_freq_real", "L0_ffn_w_freq_imag", "L0_ffn_bias"]


def kernel(**inputs):
    import numpy as _np
    import concourse.bacc as _bacc
    from concourse import mybir as _mybir
    from concourse.bass_utils import run_bass_kernel_spmd as _run

    nc = _bacc.Bacc("TRN2", target_bir_lowering=False, num_devices=1)
    arrays, args = {}, []

    def given(name, a):
        arrays[name] = a
        args.append(nc.dram_tensor(name, a.shape, _mybir.dt.from_np(a.dtype), kind="ExternalInput").ap())

    for name in _INS:
        given(f"in_{name}_dram", _np.ascontiguousarray(inputs[name]))
    width = inputs["x"].shape[-1]
    given("cos_sin_dram", _np.ascontiguousarray(tables(width).reshape(P, -1)))
    given("identity_dram", _np.eye(P, dtype=_np.float32))
    shape = inputs["x"].shape
    args.append(nc.dram_tensor("out_dram", shape, _mybir.dt.float32, kind="ExternalOutput").ap())
    xattn_ffn_kernel(nc, *args)
    r = _run(nc, [arrays], core_ids=[0])
    return r.results[0]["out_dram"]
```
